# Optimizing a Trainium2 kernel written in Bass

```python
import numpy as np
import jax
import jax.numpy as jnp

def _softmax(x, axis=-1):
    return jax.nn.softmax(x, axis=axis)

def _gelu(x):
    return jax.nn.gelu(x, approximate=True)

def _silu(x):
    return jax.nn.silu(x)

def _sigmoid(x):
    return jax.nn.sigmoid(x)

def _layernorm(x, axis=-1, eps=1e-05):
    m = jnp.mean(x, axis=axis, keepdims=True)
    v = jnp.var(x, axis=axis, keepdims=True)
    return (x - m) / jnp.sqrt(v + eps)

def _scatter_add(tgt, idx, src, axis=0):
    return tgt.at[idx].add(src)

def _segment_sum(src, seg, n):
    return jax.ops.segment_sum(src, seg, n)
kernel_name = 'mk_cond_resid_d2_seqx_r4_2b70ec'

def setup_inputs(seed: int=0):
    np.random.seed(seed)
    _w = jnp.asarray

    def _rec_inputs():
        import jax
        import jax.numpy as jnp
        _rk = jax.random.key(seed)
        x = -0.0003929 + 0.9999 * jax.random.normal(jax.random.fold_in(_rk, 1), (32, 64, 1024), jnp.float32)
        _lenS = 64 - jax.random.randint(jax.random.fold_in(_rk, 7), (32,), 0, max(1, 64 // 4) + 1, jnp.int32)
        _lenS2 = 64 - jax.random.randint(jax.random.fold_in(_rk, 8), (32,), 0, max(1, 64 // 4) + 1, jnp.int32)
        itok_B_8_3872 = jax.random.randint(jax.random.fold_in(_rk, 11), (32,), 8, 3873, jnp.int32)
        itok_B_2_6 = jax.random.randint(jax.random.fold_in(_rk, 12), (32,), 2, 7, jnp.int32)
        return (x, itok_B_8_3872, itok_B_2_6)
    x, itok_B_8_3872, itok_B_2_6 = _rec_inputs()

    def _L0_cond_setup():
        import math
        import jax, jax.numpy as jnp
        import numpy as np
        H, N, B, L = (64, 64, 16, 1024)
        DT_MIN, DT_MAX = (0.001, 0.1)

        def _get_kernel(log_dt, C, log_A_real, A_imag, length):
            Cc = C[..., 0] + 1j * C[..., 1]
            dt = jnp.exp(log_dt)
            A = -jnp.exp(log_A_real) + 1j * A_imag
            dtA = A * dt[:, None]
            P = dtA[:, :, None] * jnp.arange(length, dtype=jnp.float32)
            Cs = Cc * (jnp.exp(dtA) - 1.0) / A
            K = 2.0 * jnp.einsum('hn,hnl->hl', Cs, jnp.exp(P)).real
            return K
        key = jax.random.key(seed)
        ks = jax.random.split(key, 6)
        u = jax.random.normal(ks[0], (B, H, L), dtype=jnp.float32)
        length = jax.random.randint(ks[1], (B,), 0, L)
        log_dt = jax.random.uniform(ks[2], (H,), dtype=jnp.float32) * (math.log(DT_MAX) - math.log(DT_MIN)) + math.log(DT_MIN)
        C = jax.random.normal(ks[3], (H, N, 2), dtype=jnp.float32)
        log_A_real = jnp.log(0.5 * jnp.ones((H, N), dtype=jnp.float32))
        A_imag = math.pi * jnp.broadcast_to(jnp.arange(N, dtype=jnp.float32), (H, N))
        D = jax.random.normal(ks[4], (H,), dtype=jnp.float32)
        return {'u': u, 'length': length, 'log_dt': log_dt, 'C': C, 'log_A_real': log_A_real, 'A_imag': A_imag, 'D': D}
    _L0_cond_all = _L0_cond_setup()
    _L0_cond_in = {k: v for k, v in _L0_cond_all.items() if k in ('log_dt', 'C', 'log_A_real', 'A_imag', 'D')}
    del _L0_cond_all

    def _L1_cond_setup():
        import jax, jax.numpy as jnp
        import numpy as np
        B, N, H, F = (4, 128, 1024, 2752)
        L, R, RANK = (1, 16, 16)
        SCALE = 0.5
        key = jax.random.key(seed)
        ks = jax.random.split(key, 12)
        nrm = lambda k, shape, fan: jax.random.normal(k, shape, jnp.float32) * fan ** (-0.5)
        inp = {'x': jax.random.normal(ks[0], (B, N, H), jnp.float32), 'W_gate': nrm(ks[1], (F, H), H), 'W_up': nrm(ks[2], (F, H), H), 'W_down': nrm(ks[3], (H, F), F), 'A_gate': nrm(ks[4], (L, R, RANK, H), H), 'B_gate': nrm(ks[5], (L, R, F, RANK), RANK), 'A_up': nrm(ks[6], (L, R, RANK, H), H), 'B_up': nrm(ks[7], (L, R, F, RANK), RANK), 'A_down': nrm(ks[8], (L, R, RANK, F), F), 'B_down': nrm(ks[9], (L, R, H, RANK), RANK), 'lora_indices': jax.random.randint(ks[10], (B,), 0, R), 'layer_idx': 0}
        return inp
    _L1_cond_all = _L1_cond_setup()
    _L1_cond_in = {k: v for k, v in _L1_cond_all.items() if k in ('W_gate', 'W_up', 'W_down', 'A_gate', 'B_gate', 'A_up', 'B_up', 'A_down', 'B_down')}
    del _L1_cond_all
    return {'x': x, 'itok_B_8_3872': itok_B_8_3872, 'itok_B_2_6': itok_B_2_6, 'L0_cond_log_dt': _L0_cond_in['log_dt'], 'L0_cond_C': _L0_cond_in['C'], 'L0_cond_log_A_real': _L0_cond_in['log_A_real'], 'L0_cond_A_imag': _L0_cond_in['A_imag'], 'L0_cond_D': _L0_cond_in['D'], 'L1_cond_W_gate': _L1_cond_in['W_gate'], 'L1_cond_W_up': _L1_cond_in['W_up'], 'L1_cond_W_down': _L1_cond_in['W_down'], 'L1_cond_A_gate': _L1_cond_in['A_gate'], 'L1_cond_B_gate': _L1_cond_in['B_gate'], 'L1_cond_A_up': _L1_cond_in['A_up'], 'L1_cond_B_up': _L1_cond_in['B_up'], 'L1_cond_A_down': _L1_cond_in['A_down'], 'L1_cond_B_down': _L1_cond_in['B_down']}

def reference(x, itok_B_8_3872, itok_B_2_6, L0_cond_log_dt, L0_cond_C, L0_cond_log_A_real, L0_cond_A_imag, L0_cond_D, L1_cond_W_gate, L1_cond_W_up, L1_cond_W_down, L1_cond_A_gate, L1_cond_B_gate, L1_cond_A_up, L1_cond_B_up, L1_cond_A_down, L1_cond_B_down):
    import jax
    import jax.numpy as jnp

    def _L0_cond_ref(u, length, log_dt, C, log_A_real, A_imag, D):
        import math
        import jax, jax.numpy as jnp
        import numpy as np
        H, N, B, L = (64, 64, 16, 1024)
        DT_MIN, DT_MAX = (0.001, 0.1)

        def _get_kernel(log_dt, C, log_A_real, A_imag, length):
            Cc = C[..., 0] + 1j * C[..., 1]
            dt = jnp.exp(log_dt)
            A = -jnp.exp(log_A_real) + 1j * A_imag
            dtA = A * dt[:, None]
            P = dtA[:, :, None] * jnp.arange(length, dtype=jnp.float32)
            Cs = Cc * (jnp.exp(dtA) - 1.0) / A
            K = 2.0 * jnp.einsum('hn,hnl->hl', Cs, jnp.exp(P)).real
            return K
        Bq, Hq, Lq = u.shape
        mask = (jnp.arange(Lq) < length[:, None]).astype(u.dtype)
        u_m = u * mask[:, None, :]
        kernel = _get_kernel(log_dt, C, log_A_real, A_imag, Lq)
        n = 2 * Lq
        k_f = jnp.fft.rfft(kernel, n=n)
        u_f = jnp.fft.rfft(u_m, n=n)
        y = jnp.fft.irfft(u_f * k_f, n=n)[..., :Lq]
        y = y + u_m * D[:, None]
        return y * mask[:, None, :]

    def _L1_cond_ref(x, W_gate, W_up, W_down, A_gate, B_gate, A_up, B_up, A_down, B_down, lora_indices, layer_idx):
        import jax, jax.numpy as jnp
        import numpy as np
        B, N, H, F = (4, 128, 1024, 2752)
        L, R, RANK = (1, 16, 16)
        SCALE = 0.5

        def lora_add(base, inp, A, B):
            Ab = A[layer_idx][lora_indices]
            Bb = B[layer_idx][lora_indices]
            t = jnp.einsum('bri,bni->bnr', Ab, inp)
            return base + jnp.einsum('bor,bnr->bno', Bb, t) * SCALE
        gate = lora_add(jnp.einsum('bnh,fh->bnf', x, W_gate), x, A_gate, B_gate)
        up = lora_add(jnp.einsum('bnh,fh->bnf', x, W_up), x, A_up, B_up)
        act = jax.nn.silu(gate) * up
        down = lora_add(jnp.einsum('bnf,hf->bnh', act, W_down), act, A_down, B_down)
        return down
    x = x + _L0_cond_ref(x, itok_B_8_3872, L0_cond_log_dt, L0_cond_C, L0_cond_log_A_real, L0_cond_A_imag, L0_cond_D)
    x = x + _L1_cond_ref(x, L1_cond_W_gate, L1_cond_W_up, L1_cond_W_down, L1_cond_A_gate, L1_cond_B_gate, L1_cond_A_up, L1_cond_B_up, L1_cond_A_down, L1_cond_B_down, itok_B_2_6, 0)
    return x

_drawn_inputs = setup_inputs


def setup_inputs(seed=0):
    import zlib

    import numpy as np

    out = dict(_drawn_inputs(seed))
    spreads = {'L0_cond_log_A_real': (-0.6931471824645996, 0.2)}
    factors = {}
    for name, (base, spread) in spreads.items():
        noise = np.random.default_rng([zlib.crc32(name.encode()), seed]).standard_normal(out[name].shape)
        drawn = base * np.exp(spread * noise) if base else spread * noise
        out[name] = jnp.asarray(drawn.astype(out[name].dtype))
    for name, factor in factors.items():
        out[name] = (out[name] * factor).astype(out[name].dtype)
    return out
```

```python
from contextlib import ExitStack

import numpy as np
import concourse.bass as bass
from concourse import mybir

F32 = mybir.dt.float32
F32R = mybir.dt.float32r
I32 = mybir.dt.int32
ALU = mybir.AluOpType
ACT = mybir.ActivationFunctionType

P = 128
B, H, L = 32, 64, 1024
F = 2752
R, RANK = 16, 16
C = L // P
G = 8
BG = B // G
SW = 4
T = B * H // SW
HB = H * BG
FT = F // P
FR = F - FT * P
KT = FT + 1
NS = 64
NA = 32
KPAD = P + L
HG = 8
NG = H // HG
NTT = 4
NCV = 4

GU0 = 3
TD0 = GU0 + 2 * FT
DN0 = TD0 + 3
UNITS = DN0 + 3 * C
NSLOT = 3
UW = 10
assert UNITS % NSLOT == 0 and GU0 % NSLOT == 0 and (2 * FT) % 6 == 0
GUT = C + 1
TDT = (8, 8, 6)
DNT = (8, 8, 7)

EV_TG, EV_TU, EV_L, EV_GU, EV_TD, EV_Y = 0, 1, 2, 3, 3 + FT, 5 + FT
EVS = EV_Y + C
HIS = 4 + FT
SIL = 2 + FT
GATHERS = 17
ACS = 1 + FT

CA, CB, CPOS, CMASK, CPH, CAL, CBE, CNAL = 0, 32, 64, 72, 80, 81, 82, 83
NC_ = 84

MAGIC = 12582912.0
TWO_PI = 6.283185307179586
PI_A = 6.28125
PI_B = 1014 / 2 ** 19
PI_C = TWO_PI - PI_A - PI_B
LN_A = 0.693359375
LN_B = 0.6931471805599453 - LN_A
SIN_SCALE = float(np.nextafter(np.float32(TWO_PI), np.float32(0)))


def build(nc, xt_d, xn_d, idx_d, len_d, par_d, cst_d, wgu_d, wl_d, bgu_d, wd_d, wdl_d, bd_d,
          ag_d, au_d, ad_d, out_d):
    k_d = nc.dram_tensor("k_pad", [H, KPAD], F32, kind="Internal")
    x1_d = nc.dram_tensor("x1_keep", [P, G, C, HB], F32, kind="Internal").ap()
    bgs_d = nc.dram_tensor("bgu_sel", [SW, FT + 1, P, 2 * P], F32, kind="Internal").ap()
    bds_d = nc.dram_tensor("bd_sel", [SW, C, P, 2, P], F32, kind="Internal").ap()
    ags_d = nc.dram_tensor("a_gate_sel", [SW, P, C * P], F32, kind="Internal").ap()
    aus_d = nc.dram_tensor("a_up_sel", [SW, P, C * P], F32, kind="Internal").ap()
    ads_d = nc.dram_tensor("a_down_sel", [SW, P, KT * P], F32, kind="Internal").ap()
    k_ap = k_d.ap()

    with ExitStack() as ctx:
        START = (nc.sbuf_base + 31) // 32 * 32
        ARENA = 206 * 1024
        ctx.enter_context(nc.sbuf_tensor("arena", [P, ARENA], mybir.dt.uint8))

        class Region:
            def __init__(self, start):
                self.at = start

            def take(self, name, shape, dt=F32):
                t = nc.alloc_sbuf_tensor_at(name, [P, *shape], dt, offset=self.at)
                self.at += (int(np.prod(shape)) * 4 + 31) // 32 * 32
                assert self.at <= START + ARENA, (name, self.at)
                return t

        common = Region(START)
        raw = common.take("raw", [NSLOT, UW * P])
        whi = common.take("whi", [NSLOT, UW * P], F32R)
        wlo = common.take("wlo", [NSLOT, UW * P], F32R)
        cst = common.take("cst", [NC_])
        idx = common.take("idx", [2 * B], I32)
        a = Region(common.at)
        xt = a.take("xt", [G, C, H, BG])
        tt = a.take("tt", [NTT, L])
        xn = a.take("xn", [2, NTT, C * B])
        split_at = a.at
        par = a.take("par", [6, H])
        leni = a.take("leni", [B], I32)
        lenf = a.take("lenf", [B])
        mask = a.take("mask", [C, B])
        ctmp = a.take("ctmp", [2, C * B])
        zero = a.take("zero", [P])
        sm = {n: a.take("sm_" + n, [2 * H if n in ("z", "ek", "er", "ep", "es") else H]) for n in (
            "z", "ek", "er", "ep", "es", "dre", "dim", "r", "rc", "v", "kk", "cs", "sn", "ed", "er1", "ei",
            "nr", "ni", "u1", "u2", "u3", "u4", "ar", "den", "c1", "c2")}
        eki = a.take("eki", [2 * H], I32)
        tb = {n: a.take("tb_" + n, [HG, NA]) for n in (
            "p", "k", "f", "g", "fc", "f2", "g2", "f3", "q1", "q2", "m1", "m2", "s1", "co1", "s2", "t1", "t2",
            "gg", "e2")}
        ksb = a.take("ksb", [HG, NA])
        a_all = a.take("a_all", [KT, R * RANK])
        a_sel = a.take("a_sel", [KT * P])
        b = Region(common.at)
        acthi = b.take("acthi", [KT, T], F32R)
        actlo = b.take("actlo", [KT, T], F32R)
        b.at = max(b.at, split_at)
        xhi = b.take("xhi", [C, T], F32R)
        xlo = b.take("xlo", [C, T], F32R)
        tghi = b.take("tghi", [2, T], F32R)
        tglo = b.take("tglo", [2, T], F32R)
        sg = b.take("sg", [3, T])
        upc = b.take("upc", [T])
        atmp = b.take("atmp", [3, T])
        xstage = b.take("xstage", [2, T])
        xres = b.take("xres", [2, T])
        ostage = b.take("ostage", [2, T])

        ps = [ctx.enter_context(nc.psum_tensor(f"ps{i}", [P, 512], F32)) for i in range(8)]

        def sem(name):
            return ctx.enter_context(nc.semaphore(name))

        s_in = sem("s_in")
        s_idx = sem("s_idx")
        s_xt = sem("s_xt")
        s_xn = [sem(f"s_xn{i}") for i in range(2)]
        s_zero = sem("s_zero")
        s_zst = sem("s_zst")
        s_chain = sem("s_chain")
        s_small = sem("s_small")
        s_smallA = sem("s_smallA")
        s_arg = sem("s_arg")
        s_trig = sem("s_trig")
        s_tab = sem("s_tab")
        s_kmm = sem("s_kmm")
        s_ksb = sem("s_ksb")
        s_kst = sem("s_kst")
        s_tt = [sem(f"s_tt{i}") for i in range(NTT)]
        s_conv = sem("s_conv")
        s_cev = sem("s_cev")
        s_x1 = sem("s_x1")
        s_x1st = sem("s_x1st")
        s_bg = sem("s_bg")
        s_al = sem("s_al")
        s_acp = sem("s_acp")
        s_ast = sem("s_ast")
        s_raw = [sem(f"s_raw{i}") for i in range(NSLOT)]
        s_whi = sem("s_whi")
        s_wlo = sem("s_wlo")
        s_unit = sem("s_unit")
        s_ev = sem("s_ev")
        s_hi = sem("s_hi")
        s_sil = sem("s_sil")
        s_t = sem("s_t")
        s_act = sem("s_act")
        s_xhi = sem("s_xhi")
        s_xlo = sem("s_xlo")
        s_xst = [sem(f"s_xst{i}") for i in range(2)]
        s_xres = [sem(f"s_xres{i}") for i in range(2)]
        s_out = [sem(f"s_out{i}") for i in range(2)]

        block = ctx.enter_context(nc.Block())

        @block.sync
        def _(sp):
            sp.dma_start(idx[0:1, 0:B], idx_d).then_inc(s_idx, 16)
            sp.dma_start(cst[:, :], cst_d).then_inc(s_in, 16)
            sp.dma_start(par[:, :, :], par_d).then_inc(s_in, 16)
            sp.dma_start(leni[:, :], bass.AP(tensor=len_d.tensor, offset=0, ap=[[0, P], [1, B]])).then_inc(s_in, 16)
            for g in range(0, G, 2):
                sp.dma_start(xt[:, g:g + 2], xt_d[:, g:g + 2]).then_inc(s_xt, 16)
            sp.wait_ge(s_zero, 1)
            sp.dma_start(k_ap[:, 0:P], zero[0:H, :]).then_inc(s_zst, 16)
            sp.wait_ge(s_zst, 16)

            def toeplitz(h, slot):
                src = bass.AP(tensor=k_d, offset=h * KPAD + 1, ap=[[1, P], [1, L]])
                sp.dma_start(tt[:, slot, :], src).then_inc(s_tt[slot], 16)

            def residual(q, slot):
                sp.dma_start(xn[:, slot, :, :], xn_d[q]).then_inc(s_xn[slot], 16)

            sp.wait_ge(s_kst, 16)
            for h in range(HG):
                if h >= NTT:
                    sp.wait_ge(s_conv, h - NTT + 1)
                toeplitz(h, h % NTT)
                if h % NTT == 0:
                    residual(h // NTT, h // NTT)
            with sp.Fori(1, NG) as g:
                sp.wait_ge(s_kst, 16 * (g + 1))
                for i in range(HG):
                    sp.wait_ge(s_conv, HG * g + i - NTT + 1)
                    toeplitz(HG * g + i, i % NTT)
                    if i % NTT == 0:
                        sp.wait_ge(s_x1, HG * g + i - NTT)
                        residual(2 * g + i // NTT, i // NTT)

            def load(j, m, first, second, n0):
                slot = m % NSLOT
                if n0 is not None:
                    sp.wait_ge(s_wlo, n0 - NSLOT + 1)
                for dst, src in (first, second):
                    sp.dma_start(raw[:, slot, dst[0] * P:dst[1] * P], src).then_inc(s_raw[slot], 16)

            def head_units(j, n0):
                sp.wait_ge(s_bg, 16 * GATHERS * (j + 1))
                for m, src in ((0, ags_d), (1, aus_d)):
                    load(j, m, ((0, 4), src[j, :, 0:4 * P]), ((4, 8), src[j, :, 4 * P:8 * P]),
                         None if n0 is None else n0 + m)
                load(j, 2, ((0, 8), wl_d), ((8, 10), bgs_d[j, FT]), None if n0 is None else n0 + 2)

            def body_units(j):
                n0 = UNITS * j
                with sp.Fori(0, FT // 3) as t:
                    for q in range(6):
                        half = q % 2
                        load(j, GU0 + q,
                             ((0, 8), wgu_d[3 * t + q // 2, :, half * C * P:(half + 1) * C * P]),
                             ((8, 9), bgs_d[j, 3 * t + q // 2, :, half * P:(half + 1) * P]),
                             n0 + GU0 + 6 * t + q)
                k0 = 0
                for u, k in enumerate(TDT):
                    load(j, TD0 + u, ((0, 4), ads_d[j, :, k0 * P:(k0 + 4) * P]),
                         ((4, k), ads_d[j, :, (k0 + 4) * P:(k0 + k) * P]), n0 + TD0 + u)
                    k0 += k
                with sp.Fori(0, C) as c:
                    for u in range(3):
                        n = n0 + DN0 + 3 * c + u
                        if u < 2:
                            load(j, DN0 + u, ((0, 4), wd_d[c, :, u * 8 * P:(u * 8 + 4) * P]),
                                 ((4, 8), wd_d[c, :, (u * 8 + 4) * P:(u + 1) * 8 * P]), n)
                        else:
                            load(j, DN0 + u, ((0, 5), wd_d[c, :, 16 * P:21 * P]),
                                 ((5, 7), bds_d[j, c].rearrange("p g n -> p (g n)")), n)

            sp.wait_ge(s_ast, 16 * 3 * SW)
            head_units(0, None)
            with sp.Fori(0, SW - 1) as j:
                body_units(j)
                head_units(j + 1, UNITS * (j + 1))
            body_units(SW - 1)

        @block.gpsimd
        def _(pool):
            pool.memset(zero[:, :], 0.0).then_inc(s_zero, 1)
            pool.wait_ge(s_idx, 16)
            pool.wait_ge(s_xt, 16 * 4)

            def gather_b(j):
                pool.dma_start(bds_d[j, :, 0:FR, :, :], wdl_d).then_inc(s_bg, 16)
                for b8 in range(8):
                    r = pool.value_load(idx[0:1, bass.ds(8 * j + b8, 1)], min_val=0, max_val=R - 1)
                    pool.dma_start(bgs_d[j, :, b8 * RANK:(b8 + 1) * RANK, :], bgu_d[r]).then_inc(s_bg, 16)
                    p0 = FR + (b8 % BG) * RANK
                    pool.dma_start(bds_d[j, :, p0:p0 + RANK, b8 // BG, :], bd_d[r]).then_inc(s_bg, 16)

            gather_b(0)
            for m, (src, dst, kt) in enumerate(((ag_d, ags_d, C), (au_d, aus_d, C), (ad_d, ads_d, KT))):
                if m:
                    pool.wait_ge(s_ast, 16 * SW * m)
                pool.dma_start(a_all[:, 0:kt, :], src).then_inc(s_al, 16)
                pool.wait_ge(s_al, 16 * (m + 1))
                with pool.Fori(0, SW) as j:
                    sel = a_sel[:, 0:kt * P].rearrange("p (k n) -> p k n", n=P)
                    for b8 in range(8):
                        r = pool.value_load(idx[0:1, bass.ds(8 * j + b8, 1)], min_val=0, max_val=R - 1)
                        pool.tensor_copy(sel[:, :, b8 * RANK:(b8 + 1) * RANK],
                                         a_all[:, 0:kt, bass.ds(r * RANK, RANK)]).then_inc(s_acp, 1)
                    pool.wait_ge(s_acp, 8 * (SW * m + j + 1))
                    pool.wait_ge(s_al, 16 * (m + 1))
                    pool.dma_start(dst[j], a_sel[:, 0:kt * P]).then_inc(s_ast, 16)
                    pool.wait_ge(s_ast, 16 * (SW * m + j + 1))
                    pool.wait_ge(s_al, 16 * (m + 1))
            pool.wait_ge(s_ast, 16 * 3 * SW)

            pool.wait_ge(s_x1, H)
            for j in range(SW):
                pool.dma_start(x1_d[:, 2 * j:2 * j + 2],
                               xt[:, 2 * j:2 * j + 2].rearrange("p g c h b -> p g c (h b)")).then_inc(s_x1st, 16)
            with pool.Fori(1, SW) as j:
                pool.wait_ge(s_bg, 16 * GATHERS * j)
                pool.wait_ge(s_x1st, 16 * SW)
                gather_b(j)

        @block.tensor
        def _(pe):
            def k_group(g):
                pe.wait_ge(s_tab, g + 1)
                for i in range(HG):
                    last = nc.tensor.matmul(ps[7][0:NA, i * NA:(i + 1) * NA], tb["gg"][:, i, :], tb["e2"][:, i, :],
                                            start=True, stop=True)
                last.then_inc(s_kmm, 1)

            def conv(h, slot, wait, first=False):
                pe.wait_ge(s_tt[slot], wait)
                if not first:
                    pe.wait_ge(s_cev, h - NCV + 1)
                for d in range(C):
                    mov = xt[:, :, 0:C - d, h, :].rearrange("p g c b -> p c g b")
                    last = nc.tensor.matmul(ps[slot][:, d * B:C * B], tt[:, slot, d * P:(d + 1) * P], mov,
                                            start=(d == 0), stop=(d == C - 1), skip_group_check=True)
                last.then_inc(s_conv, 1)

            k_group(0)
            k_group(1)
            pe.wait_ge(s_xt, 16 * 4)
            for h in range(NTT):
                conv(h, h, 16, first=True)
            for h in range(NTT, HG):
                conv(h, h % NTT, 32)
            k_group(2)
            with pe.Fori(1, NG - 2) as g:
                for i in range(HG):
                    conv(HG * g + i, i % NTT, 16 * (2 * g + i // NTT + 1))
                k_group(g + 2)
            for g in (NG - 2, NG - 1):
                for i in range(HG):
                    conv(HG * g + i, i % NTT, 16 * (2 * g + i // NTT + 1))

            def passes(out, slot, k, hi, lo, start, stop, rows=P):
                w_hi = whi[0:rows, slot, k * P:(k + 1) * P]
                w_lo = wlo[0:rows, slot, k * P:(k + 1) * P]
                nc.tensor.matmul(out, w_hi, hi, start=start, stop=False, skip_group_check=True)
                nc.tensor.matmul(out, w_hi, lo, start=False, stop=False, skip_group_check=True)
                return nc.tensor.matmul(out, w_lo, hi, start=False, stop=stop, skip_group_check=True)

            def x_tiles(bank, slot, stop):
                for k in range(C):
                    last = passes(ps[bank][:, :], slot, k, xhi[:, k, :], xlo[:, k, :], k == 0, stop and k == C - 1)
                return last

            def sweep(j):
                n0 = UNITS * j
                for m in range(2):
                    pe.wait_ge(s_wlo, n0 + m + 1)
                    for k in range(C):
                        if m == 0:
                            pe.wait_ge(s_xlo, C * j + k + 1)
                        last = passes(ps[m][:, :], m, k, xhi[:, k, :], xlo[:, k, :], k == 0, k == C - 1)
                    last.then_inc(s_unit, 1)
                pe.wait_ge(s_wlo, n0 + 3)
                x_tiles(2, 2, False)
                pe.wait_ge(s_t, 3 * j + 2)
                passes(ps[2][:, :], 2, 8, tghi[:, 0, :], tglo[:, 0, :], False, False)
                passes(ps[2][:, :], 2, 9, tghi[:, 1, :], tglo[:, 1, :], False, True).then_inc(s_unit, 1)
                with pe.Fori(0, FT // 3) as t:
                    for q in range(6):
                        bank, slot = (GU0 + q) % 6, q % NSLOT
                        pe.wait_ge(s_wlo, n0 + GU0 + 6 * t + q + 1)
                        if q % 2 == 0:
                            pe.wait_ge(s_ev, EVS * j + 3 * t + q // 2 + 1)
                        x_tiles(bank, slot, False)
                        passes(ps[bank][:, :], slot, C, tghi[:, q % 2, :], tglo[:, q % 2, :],
                               False, True).then_inc(s_unit, 1)
                k0 = 0
                for u, kt in enumerate(TDT):
                    pe.wait_ge(s_wlo, n0 + TD0 + u + 1)
                    pe.wait_ge(s_act, ACS * j + min(k0 + kt + 1, ACS))
                    for k in range(kt):
                        kk, rows = k0 + k, P if k0 + k < FT else FR
                        last = passes(ps[6][:, :], u, k, acthi[0:rows, kk, :], actlo[0:rows, kk, :],
                                      kk == 0, kk == FT, rows)
                    last.then_inc(s_unit, 1)
                    k0 += kt
                def output(c, bank):
                    for u, kt in enumerate(DNT):
                        pe.wait_ge(s_wlo, n0 + DN0 + 3 * c + u + 1)
                        if u == 0:
                            pe.wait_ge(s_ev, EVS * j + EV_Y + c - 1)
                        for k in range(min(kt, FT - 8 * u)):
                            last = passes(ps[bank][:, :], u, k, acthi[:, 8 * u + k, :], actlo[:, 8 * u + k, :],
                                          u + k == 0, False)
                        if u == 2:
                            pe.wait_ge(s_t, 3 * j + 3)
                            for g in range(2):
                                cols = slice(g * HB, (g + 1) * HB)
                                last = passes(ps[bank][:, cols], u, 5 + g, acthi[:, FT, cols], actlo[:, FT, cols],
                                              False, True)
                        last.then_inc(s_unit, 1)

                with pe.Fori(0, C // 2) as c2:
                    output(2 * c2, 7)
                    output(2 * c2 + 1, 6)

            with pe.Fori(0, SW) as j:
                sweep(j)

        @block.scalar
        def _(act):
            act.wait_ge(s_small, 1)
            nc.scalar.activation(sm["sn"][:, :], sm["r"][:, :], ACT.Sin, scale=SIN_SCALE).then_inc(s_smallA, 1)
            nc.scalar.activation(sm["cs"][:, :], sm["rc"][:, :], ACT.Sin, scale=SIN_SCALE).then_inc(s_smallA, 1)

            def tables(g):
                act.wait_ge(s_arg, g + 1)
                nc.scalar.activation(tb["m1"][:], tb["q1"][:], ACT.Exp).then_inc(s_trig, 1)
                nc.scalar.activation(tb["m2"][:], tb["q2"][:], ACT.Exp).then_inc(s_trig, 1)
                nc.scalar.activation(tb["s1"][:], tb["f"][:], ACT.Sin, scale=SIN_SCALE).then_inc(s_trig, 1)
                nc.scalar.activation(tb["co1"][:], tb["fc"][:], ACT.Sin, scale=SIN_SCALE).then_inc(s_trig, 1)
                nc.scalar.activation(tb["s2"][:], tb["f3"][:], ACT.Sin, scale=SIN_SCALE).then_inc(s_trig, 1)
                act.wait_ge(s_ksb, g + 1)
                dst = k_ap[bass.ds(HG * g, HG), P:KPAD].rearrange("h (a b) -> a h b", b=NA)
                act.dma_start(dst, ksb[0:NA, :, :]).then_inc(s_kst, 16)
                act.wait_ge(s_kst, 16 * (g + 1))

            with act.Fori(0, NG) as g:
                tables(g)

            def split_hi(unit, m, cols, first=False):
                loads, n = unit
                slot = m % NSLOT
                act.wait_ge(s_raw[slot], loads)
                if not first:
                    act.wait_ge(s_unit, n - NSLOT + 1)
                nc.scalar.activation(whi[:, slot, 0:cols * P], raw[:, slot, 0:cols * P], ACT.Copy).then_inc(s_whi, 1)

            def unit(j, m, t=0):
                return (UNITS // NSLOT * 32 * j + 32 * (m // NSLOT + 1) + 64 * t, UNITS * j + m + 6 * t)

            def t_hi(j, e):
                act.wait_ge(s_ev, EVS * j + e + 1)
                nc.scalar.activation(tghi[:, e, :], atmp[:, e, :], ACT.Copy).then_inc(s_hi, 1)

            def act_hi(j, ev, k, slot, rows=P):
                act.wait_ge(s_ev, ev + 1)
                nc.scalar.activation(acthi[0:rows, bass.ds(k, 1), :].rearrange("p a n -> p (a n)"),
                                     atmp[0:rows, slot, :], ACT.Copy).then_inc(s_hi, 1)

            def x_hi(c, src):
                nc.scalar.activation(xhi[:, c, :], src, ACT.Copy).then_inc(s_xhi, 1)

            def x1_chunk(j, c):
                return x1_d[:, bass.ds(2 * j, 2), c, :]

            def by_group(tile):
                return tile.rearrange("p (g n) -> p g n", g=2)

            def residual_in(j, c):
                if c >= 2:
                    act.wait_ge(s_ev, EVS * j + EV_Y + c - 1)
                act.dma_start(by_group(xres[:, c % 2, :]), x1_chunk(j, c)).then_inc(s_xres[c % 2], 16)

            def next_x_in(j, c):
                act.wait_ge(s_xlo, C * (j + 1) + max(c - 1, 0))
                act.dma_start(by_group(xstage[:, c % 2, :]), x1_chunk(j + 1, c)).then_inc(s_xst[c % 2], 16)

            def store(j, c):
                act.wait_ge(s_ev, EVS * j + EV_Y + c + 1)
                act.dma_start(out_d[:, bass.ds(2 * j, 2), c, :],
                              by_group(ostage[:, c % 2, :])).then_inc(s_out[c % 2], 16)

            def steps_gu(j, t, look):
                for q in range(6):
                    m = GU0 + 1 + q
                    look(m + 2, t)
                    act.wait_ge(s_unit, UNITS * j + m + 6 * t)
                    i3, bank = q // 2, (GU0 + q) % 6
                    if q % 2 == 0:
                        nc.scalar.activation(sg[:, i3, :], ps[bank][:, :], ACT.Silu).then_inc(s_sil, 1)
                    else:
                        act_hi(j, EVS * j + EV_GU + 3 * t + i3, 3 * t + i3, i3)

            def sweep(j, last):
                def look(m, t=0):
                    if m < UNITS:
                        cols = (GUT if m < TD0 else TDT[m - TD0] if m < DN0 else DNT[(m - DN0) % 3])
                        split_hi(unit(j, m, t), m, cols)
                    elif not last:
                        split_hi(unit(j + 1, m - UNITS), m, C if m < UNITS + 2 else UW)

                act.wait_ge(s_unit, UNITS * j + 1)
                look(3)
                t_hi(j, 0)
                look(4)
                t_hi(j, 1)
                look(5)
                act.wait_ge(s_unit, UNITS * j + 3)
                nc.scalar.activation(sg[0:FR, 2, :], ps[2][0:FR, :], ACT.Silu).then_inc(s_sil, 1)
                nc.scalar.activation(upc[0:FR, :], ps[2][FR:P, :], ACT.Copy).then_inc(s_sil, 1)
                act.wait_ge(s_x1st, 16 * SW)
                act_hi(j, EVS * j + EV_L, FT, 2, FR)
                with act.Fori(0, FT // 3 - 1) as t:
                    steps_gu(j, t, look)
                steps_gu(j, FT // 3 - 1, lambda m, t: look(m + 6 * t))
                for m in (46, 47, 48):
                    look(m + 2)
                act.wait_ge(s_ev, EVS * j + EV_TD + 2)
                nc.scalar.activation(acthi[FR:P, FT, :], atmp[FR:P, 0, :], ACT.Copy).then_inc(s_hi, 1)
                for c in range(2):
                    residual_in(j, c)
                    if not last:
                        next_x_in(j, c)
                for c in range(C):
                    look(DN0 + 3 * c + 3)
                    if c:
                        store(j, c - 1)
                    if c and c + 1 < C:
                        residual_in(j, c + 1)
                        if not last:
                            next_x_in(j, c + 1)
                    if not last:
                        act.wait_ge(s_xst[c % 2], 16 * (C // 2) * j + 16 * (c // 2 + 1))
                        x_hi(c, xstage[:, c % 2, :])
                    for m in range(DN0 + 3 * c + 4, DN0 + 3 * c + 6):
                        look(m)
                store(j, C - 1)

            act.wait_ge(s_x1, H)
            act.wait_ge(s_ast, 16 * 3 * SW)
            for c in range(C):
                x_hi(c, xt[:, 0:2, c, :, :].rearrange("p g h b -> p g (h b)"))
                if c < NSLOT:
                    split_hi(unit(0, c), c, C if c < 2 else UW, first=True)
            with act.Fori(0, SW - 1) as j:
                sweep(j, False)
            sweep(SW - 1, True)
            for i in range(2):
                act.wait_ge(s_out[i], 16 * SW * C // 2)

        @block.vector
        def _(dve):
            V = nc.vector
            count = [0]

            def link(ins):
                count[0] += 1
                ins.then_inc(s_chain, 1)
                dve.wait_ge(s_chain, count[0])

            dve.wait_ge(s_in, 16 * 3)

            def exp(dst, z, n):
                k, r, p, s = (sm[x][:, 0:n] for x in ("ek", "er", "ep", "es"))
                link(V.tensor_scalar(p, z, 88.0, -87.0, ALU.min, ALU.max))
                link(V.tensor_scalar(k, p, 1.4426950408889634, MAGIC, ALU.mult, ALU.add))
                link(V.tensor_scalar(k, k, MAGIC, None, ALU.subtract))
                link(V.scalar_tensor_tensor(r, k, -LN_A, p, ALU.mult, ALU.add))
                link(V.scalar_tensor_tensor(r, k, -LN_B, r, ALU.mult, ALU.add))
                link(V.tensor_scalar(p, r, 1.0 / 5040, 1.0 / 720, ALU.mult, ALU.add))
                for f in (120, 24, 6, 2, 1):
                    link(V.tensor_tensor(p, p, r, ALU.mult))
                    link(V.tensor_scalar(p, p, 1.0 / f, None, ALU.add))
                link(V.tensor_tensor(p, p, r, ALU.mult))
                link(V.tensor_scalar(p, p, 1.0, None, ALU.add))
                link(V.tensor_scalar(s, k, 127.0, None, ALU.add))
                link(V.tensor_copy(eki[:, 0:n], s))
                link(V.tensor_scalar(eki[:, 0:n], eki[:, 0:n], 23, None, ALU.logical_shift_left))
                link(V.tensor_tensor(dst, p, eki[:, 0:n].bitcast(F32), ALU.mult))

            dt, are = sm["z"][:, 0:H], sm["z"][:, H:2 * H]
            exp(sm["z"][:, :], par[:, 0:2, :].rearrange("p a h -> p (a h)"), 2 * H)
            link(V.tensor_scalar(sm["ar"][:], are, -1.0, None, ALU.mult))
            link(V.tensor_tensor(sm["dre"][:], sm["ar"][:], dt, ALU.mult))
            link(V.tensor_tensor(sm["dim"][:], par[:, 2, :], dt, ALU.mult))
            kk, v, r, rc = (sm[x][:] for x in ("kk", "v", "r", "rc"))
            link(V.tensor_scalar(kk, sm["dim"][:], 1.0 / TWO_PI, MAGIC, ALU.mult, ALU.add))
            link(V.tensor_scalar(kk, kk, MAGIC, None, ALU.subtract))
            link(V.scalar_tensor_tensor(v, kk, -PI_A, sm["dim"][:], ALU.mult, ALU.add))
            link(V.scalar_tensor_tensor(v, kk, -PI_B, v, ALU.mult, ALU.add))
            link(V.scalar_tensor_tensor(v, kk, -PI_C, v, ALU.mult, ALU.add))
            link(V.tensor_scalar(v, v, 1.0 / TWO_PI, None, ALU.mult))
            link(V.tensor_scalar(kk, v, MAGIC, MAGIC, ALU.add, ALU.subtract))
            link(V.tensor_tensor(r, v, kk, ALU.subtract))
            link(V.tensor_scalar(v, r, 0.25, None, ALU.add))
            link(V.tensor_scalar(kk, v, MAGIC, MAGIC, ALU.add, ALU.subtract))
            V.tensor_tensor(rc, v, kk, ALU.subtract).then_inc(s_small, 1)
            exp(sm["ed"][:], sm["dre"][:], H)
            dve.wait_ge(s_smallA, 2)
            cr, ci = par[:, 3, :], par[:, 4, :]
            s = {n: sm[n][:] for n in sm}
            link(V.tensor_tensor(s["er1"], s["ed"], s["cs"], ALU.mult))
            link(V.tensor_scalar(s["er1"], s["er1"], 1.0, None, ALU.subtract))
            link(V.tensor_tensor(s["ei"], s["ed"], s["sn"], ALU.mult))

            def product(dr, di, ar_, ai_, br, bi, op_r, op_i):
                link(V.tensor_tensor(s["u1"], ar_, br, ALU.mult))
                link(V.tensor_tensor(s["u2"], ai_, bi, ALU.mult))
                link(V.tensor_tensor(dr, s["u1"], s["u2"], op_r))
                link(V.tensor_tensor(s["u3"], ai_, br, ALU.mult))
                link(V.tensor_tensor(s["u4"], ar_, bi, ALU.mult))
                link(V.tensor_tensor(di, s["u3"], s["u4"], op_i))

            product(s["nr"], s["ni"], cr, ci, s["er1"], s["ei"], ALU.subtract, ALU.add)
            link(V.tensor_tensor(s["u1"], s["ar"], s["ar"], ALU.mult))
            link(V.tensor_tensor(s["u2"], par[:, 2, :], par[:, 2, :], ALU.mult))
            link(V.tensor_tensor(s["den"], s["u1"], s["u2"], ALU.add))
            link(V.reciprocal(s["den"], s["den"]))
            product(s["er1"], s["ei"], s["nr"], s["ni"], s["ar"], par[:, 2, :], ALU.add, ALU.subtract)
            link(V.tensor_tensor(s["er1"], s["er1"], s["den"], ALU.mult))
            link(V.tensor_tensor(s["ei"], s["ei"], s["den"], ALU.mult))
            al, be, nal = (cst[:, x:x + 1] for x in (CAL, CBE, CNAL))
            link(V.tensor_scalar(s["u1"], s["ei"], be, None, ALU.mult))
            link(V.scalar_tensor_tensor(s["c1"], s["er1"], al, s["u1"], ALU.mult, ALU.add))
            link(V.tensor_scalar(s["u1"], s["er1"], be, None, ALU.mult))
            link(V.scalar_tensor_tensor(s["c2"], s["ei"], nal, s["u1"], ALU.mult, ALU.add))
            link(V.tensor_copy(lenf[:, :], leni[:, :]))
            for c in range(C):
                link(V.tensor_scalar(mask[:, c, :], lenf[:, :], cst[:, CPOS + c:CPOS + c + 1], None, ALU.is_gt))
            prologue = count[0]

            def over_steps(x, g):
                return x[:, bass.ds(HG * g, HG)].unsqueeze(2).broadcast_to([P, HG, NA])

            def over_heads(col):
                return cst[:, col:col + NA].unsqueeze(1).broadcast_to([P, HG, NA])

            STEPS = 18

            def tables(g, wait_prev):
                done = [0]

                def step(ins):
                    ins.then_inc(s_chain, 1)
                    done[0] += 1
                    dve.wait_ge(s_chain, prologue + STEPS * g + done[0])

                t = {n: tb[n][:] for n in tb}
                for col, f in ((CA, "f"), (CB, "f2")):
                    step(V.tensor_tensor(t["p"], over_steps(sm["r"], g), over_heads(col), ALU.mult))
                    step(V.tensor_scalar(t["k"], t["p"], MAGIC, MAGIC, ALU.add, ALU.subtract))
                    step(V.tensor_tensor(t[f], t["p"], t["k"], ALU.subtract))
                for src, ph, tmp, dst in (("f", 0.25, "g", "fc"), ("f2", cst[:, CPH:CPH + 1], "g2", "f3")):
                    step(V.tensor_scalar(t[tmp], t[src], ph, None, ALU.add))
                    step(V.tensor_scalar(t["k"], t[tmp], MAGIC, MAGIC, ALU.add, ALU.subtract))
                    step(V.tensor_tensor(t[dst], t[tmp], t["k"], ALU.subtract))
                step(V.tensor_tensor(t["q1"], over_steps(sm["dre"], g), over_heads(CA), ALU.mult))
                V.tensor_tensor(t["q2"], over_steps(sm["dre"], g), over_heads(CB), ALU.mult).then_inc(s_arg, 1)
                dve.wait_ge(s_trig, 5 * g + 5)
                step(V.tensor_tensor(t["t1"], t["co1"], over_steps(sm["c1"], g), ALU.mult))
                step(V.tensor_tensor(t["t2"], t["s1"], over_steps(sm["c2"], g), ALU.mult))
                step(V.tensor_tensor(t["t1"], t["t1"], t["t2"], ALU.add))
                if wait_prev:
                    dve.wait_ge(s_kmm, g)
                step(V.tensor_tensor(t["gg"], t["t1"], t["m1"], ALU.mult))
                V.tensor_tensor(t["e2"], t["s2"], t["m2"], ALU.mult).then_inc(s_tab, 1)

            def k_out(g, wait_store):
                dve.wait_ge(s_kmm, g + 1)
                if wait_store:
                    dve.wait_ge(s_kst, 16 * g)
                kf = ksb[0:NA, :, :].rearrange("p h b -> p (h b)")
                V.tensor_copy(kf, ps[7][0:NA, 0:HG * NA]).then_inc(s_chain, 1)
                dve.wait_ge(s_chain, prologue + STEPS * g + STEPS)
                dst = ksb[0:1, :, 0:1].rearrange("p h b -> p (h b)")
                V.tensor_tensor(dst, dst, par[0:1, 5, bass.ds(HG * g, HG)], ALU.add).then_inc(s_ksb, 1)

            def evacuate(h, slot, quad, loads):
                tmp = ctmp[:, slot % 2, :]
                dve.wait_ge(s_conv, h + 1)
                V.tensor_tensor(tmp, ps[slot][:, 0:C * B], mask[:].rearrange("p c b -> p (c b)"),
                                ALU.mult).then_inc(s_cev, 1)
                dve.wait_ge(s_cev, h + 1)
                x = xt[:, :, :, h, :].rearrange("p g c b -> p c g b")
                if slot == 0:
                    dve.wait_ge(s_xn[quad], loads)
                V.tensor_tensor(x, xn[:, quad, slot, :].rearrange("p (c g b) -> p c g b", c=C, g=G),
                                tmp.rearrange("p (c g b) -> p c g b", c=C, g=G), ALU.add).then_inc(s_x1, 1)

            tables(0, False)
            k_out(0, False)
            tables(1, True)
            k_out(1, True)
            dve.wait_ge(s_xt, 16 * 4)
            with dve.Fori(0, NG - 2) as g:
                for i in range(NTT):
                    evacuate(HG * g + i, i, 0, 16 * (g + 1))
                tables(g + 2, True)
                for i in range(NTT, HG):
                    evacuate(HG * g + i, i % NTT, 1, 16 * (g + 1))
                k_out(g + 2, True)
            with dve.Fori(NG - 2, NG) as g:
                for i in range(HG):
                    evacuate(HG * g + i, i % NTT, i // NTT, 16 * (g + 1))

            def split_lo(n, m, cols):
                slot = m % NSLOT
                dve.wait_ge(s_whi, n + 1)
                V.tensor_tensor(wlo[:, slot, 0:cols * P], raw[:, slot, 0:cols * P],
                                whi[:, slot, 0:cols * P].bitcast(F32), ALU.subtract).then_inc(s_wlo, 1)

            def x_lo(n, c, src):
                dve.wait_ge(s_xhi, n)
                V.tensor_tensor(xlo[:, c, :], src, xhi[:, c, :].bitcast(F32), ALU.subtract).then_inc(s_xlo, 1)

            lmask = cst[:, CMASK:CMASK + 8].rearrange("p (g b) -> p g b", g=2)

            def evac_t(j, m):
                dve.wait_ge(s_unit, UNITS * j + m + 1)
                for g in range(2):
                    cols = slice(g * HB, (g + 1) * HB)
                    ins = V.tensor_tensor(atmp[:, m, cols].rearrange("p (h b) -> p h b", b=BG),
                                          ps[m][:, cols].rearrange("p (h b) -> p h b", b=BG),
                                          lmask[:, g:g + 1, :].broadcast_to([P, H, BG]), ALU.mult)
                ins.then_inc(s_ev, 1)
                dve.wait_ge(s_hi, HIS * j + m + 1)
                V.tensor_tensor(tglo[:, m, :], atmp[:, m, :], tghi[:, m, :].bitcast(F32),
                                ALU.subtract).then_inc(s_t, 1)

            def act_lo(hi_count, k, slot, rows=P):
                dve.wait_ge(s_hi, hi_count)
                one = bass.ds(k, 1)
                V.tensor_tensor(actlo[0:rows, one, :].rearrange("p a n -> p (a n)"), atmp[0:rows, slot, :],
                                acthi[0:rows, one, :].rearrange("p a n -> p (a n)").bitcast(F32),
                                ALU.subtract).then_inc(s_act, 1)

            def steps_gu(j, t, look):
                for q in range(6):
                    m = GU0 + 1 + q
                    look(m + 2, t)
                    if q % 2:
                        i3, bank = q // 2, (GU0 + q) % 6
                        dve.wait_ge(s_unit, UNITS * j + m + 6 * t)
                        dve.wait_ge(s_sil, SIL * j + 2 + 3 * t + i3 + 1)
                        V.tensor_tensor(atmp[:, i3, :], sg[:, i3, :], ps[bank][:, :], ALU.mult).then_inc(s_ev, 1)
                        act_lo(HIS * j + 3 + 3 * t + i3 + 1, 3 * t + i3, i3)

            def sweep(j, last):
                def look(m, t=0):
                    if m < UNITS:
                        cols = (GUT if m < TD0 else TDT[m - TD0] if m < DN0 else DNT[(m - DN0) % 3])
                        split_lo(UNITS * j + m + 6 * t, m, cols)
                    elif not last:
                        split_lo(UNITS * j + m, m, C if m < UNITS + 2 else UW)

                look(3)
                evac_t(j, 0)
                look(4)
                evac_t(j, 1)
                look(5)
                dve.wait_ge(s_sil, SIL * j + 2)
                V.tensor_tensor(atmp[0:FR, 2, :], sg[0:FR, 2, :], upc[0:FR, :], ALU.mult).then_inc(s_ev, 1)
                act_lo(HIS * j + 3, FT, 2, FR)
                with dve.Fori(0, FT // 3 - 1) as t:
                    steps_gu(j, t, look)
                steps_gu(j, FT // 3 - 1, lambda m, t: look(m + 6 * t))
                for m in (46, 47, 48):
                    look(m + 2)
                dve.wait_ge(s_unit, UNITS * j + DN0)
                for g in range(2):
                    rows, cols = slice(g * FR, (g + 1) * FR), slice(g * HB, (g + 1) * HB)
                    V.tensor_tensor(atmp[FR:P, 0, cols].rearrange("p (h b) -> p h b", b=BG),
                                    ps[6][rows, cols].rearrange("p (h b) -> p h b", b=BG),
                                    lmask[rows, g:g + 1, :].broadcast_to([FR, H, BG]), ALU.mult).then_inc(s_ev, 1)
                dve.wait_ge(s_hi, HIS * j + HIS)
                V.tensor_tensor(actlo[FR:P, FT, :], atmp[FR:P, 0, :], acthi[FR:P, FT, :].bitcast(F32),
                                ALU.subtract).then_inc(s_t, 1)
                for c in range(C):
                    if not last:
                        x_lo(C * (j + 1) + c + 1, c, xstage[:, c % 2, :])
                    for m in range(DN0 + 3 * c + 3, DN0 + 3 * c + 6):
                        look(m)
                    dve.wait_ge(s_unit, UNITS * j + DN0 + 3 * c + 3)
                    dve.wait_ge(s_xres[c % 2], 16 * (C // 2) * j + 16 * (c // 2 + 1))
                    if c >= 2:
                        dve.wait_ge(s_out[c % 2], 16 * (C // 2) * j + 16 * (c // 2))
                    V.tensor_tensor(ostage[:, c % 2, :], ps[7 - c % 2][:, :], xres[:, c % 2, :],
                                    ALU.add).then_inc(s_ev, 1)
                if not last:
                    for i in range(2):
                        dve.wait_ge(s_out[i], 16 * (C // 2) * (j + 1))

            dve.wait_ge(s_x1, H)
            for c in range(C):
                x_lo(c + 1, c, xt[:, 0:2, c, :, :].rearrange("p g h b -> p g (h b)"))
                if c < NSLOT:
                    split_lo(c, c, C if c < 2 else UW)
            with dve.Fori(0, SW - 1) as j:
                sweep(j, False)
            sweep(SW - 1, True)


def constants():
    p = np.arange(P)
    cst = np.zeros((P, NC_), np.float32)
    cst[:, CA:CA + NA] = NA * np.arange(NA)
    cst[:, CB:CB + NA] = np.arange(NA)
    cst[:, CPOS:CPOS + C] = P * np.arange(C)[None, :] + p[:, None]
    cst[:, CMASK:CMASK + 8] = 0.5 * (p[:, None] // RANK == np.arange(8)[None, :])
    cst[:, CPH] = np.where(p < NS, 0.25, 0.0)
    cst[:, CAL] = np.where(p < NS, 2.0, 0.0)
    cst[:, CBE] = np.where(p < NS, 0.0, -2.0)
    cst[:, CNAL] = -cst[:, CAL]
    return cst


def layouts(x, itok_B_8_3872, itok_B_2_6, L0_cond_log_dt, L0_cond_C, L0_cond_log_A_real, L0_cond_A_imag,
            L0_cond_D, L1_cond_W_gate, L1_cond_W_up, L1_cond_W_down, L1_cond_A_gate, L1_cond_B_gate,
            L1_cond_A_up, L1_cond_B_up, L1_cond_A_down, L1_cond_B_down):
    c = np.ascontiguousarray
    a = {}
    xs = np.asarray(x).reshape(G, BG, H, C, P).transpose(4, 0, 3, 2, 1)
    a["xt"] = c(xs[::-1])
    a["xn"] = c(xs.transpose(3, 0, 2, 1, 4).reshape(H // NTT, NTT, P, C * B).transpose(0, 2, 1, 3))
    a["idx"] = c(np.asarray(itok_B_2_6).reshape(1, B))
    a["len"] = c(np.asarray(itok_B_8_3872).reshape(1, B))
    rows = lambda v: np.broadcast_to(np.asarray(v)[None, :], (P, H))
    twice = lambda m: np.concatenate([np.asarray(m).T, np.asarray(m).T], 0)
    Cc = np.asarray(L0_cond_C)
    a["par"] = c(np.stack([rows(L0_cond_log_dt), twice(L0_cond_log_A_real), twice(L0_cond_A_imag),
                           twice(Cc[..., 0]), twice(Cc[..., 1]), rows(L0_cond_D)], 1))
    a["cst"] = constants()
    FW = FT * P
    tiles = lambda w: np.asarray(w)[:FW].reshape(FT, P, C, P).transpose(0, 3, 2, 1).reshape(FT, P, C * P)
    wg, wu = np.asarray(L1_cond_W_gate), np.asarray(L1_cond_W_up)
    a["wgu"] = c(np.concatenate([tiles(wg), tiles(wu)], 2))
    rest = lambda w: w[FW:].reshape(FR, C, P).transpose(2, 1, 0)
    a["wl"] = c(np.concatenate([rest(wg), rest(wu)], 2).reshape(P, C * P))
    bg, bu = (np.asarray(v)[0].transpose(0, 2, 1) for v in (L1_cond_B_gate, L1_cond_B_up))
    bgu = np.zeros((R, FT + 1, RANK, 2 * P), np.float32)
    for n, v in enumerate((bg, bu)):
        bgu[:, :FT, :, n * P:(n + 1) * P] = v[:, :, :FW].reshape(R, RANK, FT, P).transpose(0, 2, 1, 3)
    bgu[:, FT, :, 0:FR] = bg[:, :, FW:]
    bgu[:, FT, :, P + FR:2 * P] = bu[:, :, FW:]
    a["bgu"] = bgu
    wd = np.asarray(L1_cond_W_down)
    a["wd"] = c(wd[:, :FW].reshape(C, P, FT, P).transpose(0, 3, 2, 1).reshape(C, P, FT * P))
    wdl = wd[:, FW:].reshape(C, P, FR).transpose(0, 2, 1)
    a["wdl"] = c(np.stack([wdl, wdl], 2))
    bd = np.asarray(L1_cond_B_down)[0]
    a["bd"] = c(bd.reshape(R, C, P, RANK).transpose(0, 1, 3, 2))
    amat = lambda v: np.asarray(v)[0].reshape(R * RANK, C, P).transpose(2, 1, 0)
    a["ag"], a["au"] = c(amat(L1_cond_A_gate)), c(amat(L1_cond_A_up))
    ad = np.zeros((P, KT, R * RANK), np.float32)
    v = np.asarray(L1_cond_A_down)[0].reshape(R * RANK, F)
    ad[:, :FT] = v[:, :FW].reshape(R * RANK, FT, P).transpose(2, 1, 0)
    ad[:FR, FT] = v[:, FW:].T
    a["ad"] = ad
    return a


ORDER = ("xt", "xn", "idx", "len", "par", "cst", "wgu", "wl", "bgu", "wd", "wdl", "bd", "ag", "au", "ad")


def kernel(**inputs):
    import concourse.bacc as bacc
    from concourse.bass_utils import run_bass_kernel_spmd
    arrays = layouts(**inputs)
    nc = bacc.Bacc("TRN2", target_bir_lowering=False, num_devices=1)
    args = [nc.dram_tensor(n, arrays[n].shape, mybir.dt.from_np(arrays[n].dtype), kind="ExternalInput").ap()
            for n in ORDER]
    out = nc.dram_tensor("out", (P, G, C, HB), F32, kind="ExternalOutput").ap()
    build(nc, *args, out)
    r = run_bass_kernel_spmd(nc, [arrays], core_ids=[0])
    y = r.results[0]["out"].reshape(P, G, C, H, BG)
    return np.ascontiguousarray(y.transpose(1, 4, 3, 2, 0)).reshape(B, H, L)
```

```python
from contextlib import ExitStack

import numpy as np
import concourse.bass as bass
from concourse import mybir

F32 = mybir.dt.float32
F32R = mybir.dt.float32r
I32 = mybir.dt.int32
ALU = mybir.AluOpType
ACT = mybir.ActivationFunctionType

P = 128
B, H, L = 32, 64, 1024
F = 2752
R, RANK = 16, 16
C = L // P
G = 8
BG = B // G
SW = 4
T = B * H // SW
FT = F // P
FR = F - FT * P
KT = FT + 1
NS = 64
NA = 32
HQ, HH = 4, 16
HT = HH * BG
KPAD = P + L
HG = 8
NG = H // HG
NTT = 8
NCV = 4

GU0 = 3
TD0 = GU0 + 2 * FT
DN0 = TD0 + 3
UNITS = DN0 + 3 * C
NSLOT = 3
UW = C + 2
assert UNITS % NSLOT == 0 and GU0 % NSLOT == 0 and (2 * FT) % 6 == 0
TDT = (8, 8, 6)
DNT = (8, 8, 7)
AK = 24


def tiles_of(m):
    if m < 2:
        return C
    return UW if m < TD0 else TDT[m - TD0] if m < DN0 else DNT[(m - DN0) % 3]


def loads_of(m):
    if m < GU0:
        return 32
    if m < TD0:
        return 32 + 48 * ((m - GU0) // NSLOT + 1)
    return 32 + 48 * (2 * FT // NSLOT) + 32 * ((m - TD0) // NSLOT + 1)


LOADS = loads_of(UNITS - 1)

EV_T, EV_L, EV_GU, EV_TD, EV_Y = 0, 1, 2, 2 + FT, 4 + FT
EVS = EV_Y + C
HIS = 3 + FT
SIL = 3 + FT
GATHERS = 25
ACS = 1 + FT

CAB, CPH, CPOS, CMASK, CAL, CBE, CNAL = 0, 64, 128, 136, 140, 141, 142
NC_ = 143

MAGIC = 12582912.0
TWO_PI = 6.283185307179586
PI_A = 6.28125
PI_B = 1014 / 2 ** 19
PI_C = TWO_PI - PI_A - PI_B
LN_A = 0.693359375
LN_B = 0.6931471805599453 - LN_A
SIN_SCALE = float(np.nextafter(np.float32(TWO_PI), np.float32(0)))


def of_group(tile, g):
    return tile.rearrange("p (q g n) -> p q g n", q=HQ, g=2)[:, :, g, :]


def build(nc, xt_d, xn_d, idx_d, len_d, par_d, cst_d, wgu_d, wl_d, bgu_d, bl_d, wd_d, wdl_d, bd_d,
          agu_d, ad_d, out_d):
    def scratch(name, shape):
        return nc.dram_tensor(name, shape, F32, kind="Internal").ap()

    k_d = nc.dram_tensor("k_pad", [H, KPAD], F32, kind="Internal")
    k_ap = k_d.ap()
    y1_d = scratch("conv_out", [P, SW, HQ, C, T // HQ])
    x1_d = scratch("x1_keep", [P, SW, C, T])
    bgs_d = scratch("bgu_sel", [SW, FT, FR, 2, 2, P])
    bls_d = scratch("bl_sel", [SW, P, 2, P])
    bds_d = scratch("bd_sel", [SW, C, P, 2, P])
    ags_d = scratch("a_gu_sel", [SW, 2, P, C, P])
    ads_d = scratch("a_down_sel", [SW, P, AK, P])

    with ExitStack() as ctx:
        START = (nc.sbuf_base + 31) // 32 * 32
        ARENA = 206 * 1024
        ctx.enter_context(nc.sbuf_tensor("arena", [P, ARENA], mybir.dt.uint8))

        class Region:
            def __init__(self, start):
                self.at = start

            def take(self, name, shape, dt=F32):
                t = nc.alloc_sbuf_tensor_at(name, [P, *shape], dt, offset=self.at)
                self.at += (int(np.prod(shape)) * 4 + 31) // 32 * 32
                assert self.at <= START + ARENA, (name, self.at - START)
                return t

        common = Region(START)
        raw = common.take("raw", [NSLOT, UW * P])
        whi = common.take("whi", [NSLOT, UW * P], F32R)
        wlo = common.take("wlo", [NSLOT, UW * P], F32R)
        cst = common.take("cst", [NC_])
        idx = common.take("idx", [B], I32)
        a_all = common.take("a_all", [4, R * RANK])
        a_sel = common.take("a_sel", [2, 4 * P])
        y1s = common.take("y1s", [2, T])
        xns = common.take("xns", [2, T])
        ACT_FIRST = 6
        a = Region(common.at)
        par = a.take("par", [6, H])
        leni = a.take("leni", [B], I32)
        lenf = a.take("lenf", [B])
        mask = a.take("mask", [C, B])
        zero = a.take("zero", [P])
        eki = a.take("eki", [2 * H], I32)
        wide = ("z", "ek", "er", "ep", "ang", "angk", "trig")
        sm = {n: a.take("sm_" + n, [2 * H if n in wide else H]) for n in wide + (
            "dre", "dim", "v", "kk", "ed", "e2k", "e2r", "e2p", "er1", "ei", "qr", "qi",
            "u1", "u2", "u3", "u4", "rden", "cr", "ci", "c1", "c2")}
        assert a.at <= common.at + ACT_FIRST * 2 * T * 4
        a.at = common.at + ACT_FIRST * 2 * T * 4
        xt = a.take("xt", [HQ, C, G, HT])
        tt = a.take("tt", [NTT, L])
        tb = {n: a.take("tb_" + n, [HG, 2 * NA]) for n in ("p", "k", "f", "g", "f3", "q", "m", "tr")}
        th = {n: a.take("th_" + n, [HG, NA]) for n in ("s1", "t1", "t2", "gg", "e2")}
        ksb = a.take("ksb", [HG, NA])
        b = Region(common.at)
        acts = b.take("acts", [KT, 2, T], F32R)
        xhi = b.take("xhi", [C, T], F32R)
        xlo = b.take("xlo", [C, T], F32R)
        thi = b.take("thi", [T], F32R)
        tlo = b.take("tlo", [T], F32R)
        ts = b.take("ts", [2, T], F32R)
        tz = b.take("tz", [2, T], F32R)
        sg = b.take("sg", [3, T])
        xres = b.take("xres", [2, T])

        ps = [ctx.enter_context(nc.psum_tensor(f"ps{i}", [P, 512], F32)) for i in range(8)]

        def sem(name):
            return ctx.enter_context(nc.semaphore(name))

        s_in = sem("s_in")
        s_idx = sem("s_idx")
        s_xt0 = sem("s_xt0")
        s_xt = sem("s_xt")
        s_zero = sem("s_zero")
        s_zst = sem("s_zst")
        s_chain = sem("s_chain")
        s_len = sem("s_len")
        s_tz = sem("s_tz")
        s_small = sem("s_small")
        s_smallA = sem("s_smallA")
        s_arg = sem("s_arg")
        s_trig = sem("s_trig")
        s_tab = sem("s_tab")
        s_kmm = sem("s_kmm")
        s_ksb = sem("s_ksb")
        s_kst = sem("s_kst")
        s_tt = [sem(f"s_tt{i}") for i in range(NTT)]
        s_conv = sem("s_conv")
        s_cev = sem("s_cev")
        s_y1st = sem("s_y1st")
        s_bg = sem("s_bg")
        s_acp = sem("s_acp")
        s_piece = sem("s_piece")
        s_raw = [sem(f"s_raw{i}") for i in range(NSLOT)]
        s_whi = sem("s_whi")
        s_wlo = sem("s_wlo")
        s_tdh = sem("s_tdh")
        s_tdl = sem("s_tdl")
        s_unit = sem("s_unit")
        s_ev = sem("s_ev")
        s_hi = sem("s_hi")
        s_sil = sem("s_sil")
        s_t = sem("s_t")
        s_tsa = sem("s_tsa")
        s_tsd = sem("s_tsd")
        s_td = sem("s_td")
        s_act = sem("s_act")
        s_y1 = [sem(f"s_y1{i}") for i in range(2)]
        s_xn = [sem(f"s_xn{i}") for i in range(2)]
        s_xsum = sem("s_xsum")
        s_xhi = sem("s_xhi")
        s_xlo = sem("s_xlo")
        s_x1st = [sem(f"s_x1st{i}") for i in range(2)]
        s_xres = [sem(f"s_xres{i}") for i in range(2)]
        s_out = [sem(f"s_out{i}") for i in range(2)]

        block = ctx.enter_context(nc.Block())

        @block.sync
        def _(sp):
            sp.dma_start(par[:, :, :], par_d).then_inc(s_in, 16)
            sp.dma_start(cst[:, :], cst_d).then_inc(s_in, 16)
            sp.dma_start(idx[0:1, 0:B], idx_d).then_inc(s_idx, 16)
            sp.dma_start(leni[:, :], bass.AP(tensor=len_d.tensor, offset=0, ap=[[0, P], [1, B]])).then_inc(s_in, 16)
            sp.wait_ge(s_zero, 1)
            sp.dma_start(k_ap[:, 0:P], zero[0:H, :]).then_inc(s_zst, 16)
            sp.dma_start(xt[:, 0], xt_d[:, 0]).then_inc(s_xt0, 16)
            for q in range(1, HQ):
                sp.dma_start(xt[:, q], xt_d[:, q]).then_inc(s_xt, 16)
            sp.wait_ge(s_zst, 16)

            def toeplitz(h, slot):
                src = bass.AP(tensor=k_d, offset=h * KPAD + 1, ap=[[1, P], [1, L]])
                sp.dma_start(tt[:, slot, :], src).then_inc(s_tt[slot], 16)

            sp.wait_ge(s_kst, 16)
            for h in range(HG):
                toeplitz(h, h)
            with sp.Fori(1, NG) as g:
                sp.wait_ge(s_kst, 16 * (g + 1))
                for i in range(HG):
                    sp.wait_ge(s_conv, HG * (g - 1) + i + 1)
                    toeplitz(HG * g + i, i)

            def load(m, n, *parts):
                slot = m % NSLOT
                if n is not None:
                    sp.wait_ge(s_wlo, n - NSLOT + 1)
                for rows, t0, t1, src in parts:
                    sp.dma_start(raw[rows[0]:rows[1], slot, t0 * P:t1 * P], src).then_inc(s_raw[slot], 16)

            ALL = (0, P)

            def flat(x):
                return x.rearrange("p a n -> p (a n)")

            def head_units(j, n0):
                for g in range(2):
                    load(g, None if n0 is None else n0 + g, (ALL, 0, 4, flat(ags_d[j, g, :, 0:4])),
                         (ALL, 4, 8, flat(ags_d[j, g, :, 4:8])))
                sp.wait_ge(s_bg, 16 * GATHERS * (j + 1))
                load(2, None if n0 is None else n0 + 2, (ALL, 0, 8, wl_d), (ALL, 8, 10, flat(bls_d[j])))

            def body_units(j):
                n0 = UNITS * j
                with sp.Fori(0, FT // 3) as t:
                    for q in range(6):
                        i, half = 3 * t + q // 2, q % 2
                        sel = flat(bgs_d[j, i, :, half])
                        load(GU0 + q, n0 + GU0 + 6 * t + q,
                             (ALL, 0, 8, wgu_d[i, :, half * C * P:(half + 1) * C * P]),
                             ((0, FR), 8, 10, sel), ((FR, P), 8, 10, sel))
                sp.wait_ge(s_piece, 16 * (SW + 1) * (4 + 6))
                k0 = 0
                for u, k in enumerate(TDT):
                    load(TD0 + u, n0 + TD0 + u, (ALL, 0, 4, flat(ads_d[j, :, k0:k0 + 4])),
                         (ALL, 4, k, flat(ads_d[j, :, k0 + 4:k0 + k])))
                    k0 += k
                with sp.Fori(0, C) as c:
                    n = n0 + DN0 + 3 * c
                    for u in range(2):
                        load(DN0 + u, n + u, *((ALL, 4 * v, 4 * v + 4,
                                                wd_d[c, :, (8 * u + 4 * v) * P:(8 * u + 4 * v + 4) * P])
                                               for v in range(2)))
                    load(DN0 + 2, n + 2, (ALL, 0, 5, wd_d[c, :, 16 * P:21 * P]), (ALL, 5, 7, flat(bds_d[j, c])))

            sp.wait_ge(s_piece, 16 * ((SW + 1) * 4 + 1))
            head_units(0, None)
            with sp.Fori(0, SW - 1) as j:
                body_units(j)
                head_units(j + 1, UNITS * (j + 1))
            body_units(SW - 1)

        @block.gpsimd
        def _(pool):
            pool.memset(zero[:, :], 0.0).then_inc(s_zero, 1)
            pool.wait_ge(s_idx, 16)

            def adapter(j, b8):
                return pool.value_load(idx[0:1, bass.ds(8 * j + b8, 1)], min_val=0, max_val=R - 1)

            def gather_b(j):
                pool.dma_start(bds_d[j, :, 0:FR, :, :], wdl_d).then_inc(s_bg, 16)
                for b8 in range(8):
                    r, g, r0 = adapter(j, b8), b8 // BG, (b8 % BG) * RANK
                    pool.dma_start(bls_d[j].rearrange("(w p) g n -> w p g n", w=2)[:, r0:r0 + RANK, g, :],
                                   bl_d[r]).then_inc(s_bg, 16)
                    pool.dma_start(bgs_d[j, :, r0:r0 + RANK, :, g, :], bgu_d[r]).then_inc(s_bg, 16)
                    pool.dma_start(bds_d[j, :, FR + r0:FR + r0 + RANK, g, :], bd_d[r]).then_inc(s_bg, 16)

            def gather_a(pieces, done, source, copy, target):
                with pool.Fori(0, pieces) as c:
                    pool.dma_start(a_all[:, :, :], source(c)).then_inc(s_piece, 16)
                    rounds = SW * (done + c)
                    with pool.Fori(0, SW // 2) as j2:
                        pool.wait_ge(s_piece, 16 * (rounds + done + c + 1))
                        for i in range(2):
                            j = 2 * j2 + i
                            for b8 in range(8):
                                copy(i, adapter(j, b8), b8 // BG, (b8 % BG) * RANK).then_inc(s_acp, 1)
                            pool.wait_ge(s_acp, 8 * (rounds + j + 1))
                            pool.wait_ge(s_piece, 16 * (rounds + done + c + j + 1))
                            pool.wait_ge(s_idx, 16)
                            target(i, j, c).then_inc(s_piece, 16)

            gather_b(0)
            sel_gu = [a_sel[:, i, :].rearrange("p (g k w n) -> p g k w n", g=2, k=2, w=2) for i in range(2)]
            all_gu = a_all[:, :, :].rearrange("p (k w) n -> p k w n", k=2)
            gather_a(4, 0, lambda c: agu_d[:, bass.ds(4 * c, 4), :],
                     lambda i, r, g, r0: pool.tensor_copy(sel_gu[i][:, g, :, :, r0:r0 + RANK],
                                                          all_gu[:, :, :, bass.ds(r * RANK, RANK)]),
                     lambda i, j, c: pool.dma_start(
                         ags_d[j, :, :, bass.ds(2 * c, 2), :].rearrange("g p k n -> p g (k n)"),
                         a_sel[:, i, :].rearrange("p (g n) -> p g n", g=2)))
            sel_d = [a_sel[:, i, :].rearrange("p (k g n) -> p k g n", k=4, g=2) for i in range(2)]
            gather_a(AK // 4, 4, lambda c: ad_d[:, bass.ds(4 * c, 4), :],
                     lambda i, r, g, r0: pool.tensor_copy(sel_d[i][:, :, g, r0:r0 + RANK],
                                                          a_all[:, :, bass.ds(r * RANK, RANK)]),
                     lambda i, j, c: pool.dma_start(ads_d[j, :, bass.ds(4 * c, 4), :],
                                                    a_sel[:, i, :].rearrange("p (k n) -> p k n", k=4)))
            with pool.Fori(1, SW) as j:
                pool.wait_ge(s_bg, 16 * GATHERS * j)
                pool.wait_ge(s_idx, 16)
                gather_b(j)

        @block.tensor
        def _(pe):
            def k_group(g):
                pe.wait_ge(s_tab, g + 1)
                for i in range(HG):
                    last = nc.tensor.matmul(ps[7][0:NA, i * NA:(i + 1) * NA], th["gg"][:, i, :],
                                            th["e2"][:, i, :], start=True, stop=True)
                last.then_inc(s_kmm, 1)

            def conv(hq, i, first=False):
                slot, bank = i % NTT, i % NCV
                pe.wait_ge(s_tt[slot], 16 * (2 * hq + i // NTT + 1))
                if not first:
                    pe.wait_ge(s_cev, HH * hq + i - NCV + 1)
                for d in range(C):
                    mov = xt[:, bass.ds(hq, 1), 0:C - d, :, i * BG:(i + 1) * BG].rearrange(
                        "p q c g b -> p (q c) g b")
                    last = nc.tensor.matmul(ps[bank][:, d * B:C * B], tt[:, slot, d * P:(d + 1) * P], mov,
                                            start=(d == 0), stop=(d == C - 1), skip_group_check=True)
                last.then_inc(s_conv, 1)

            def sixteen(hq, first=False, tables=True):
                for half in range(2):
                    for i in range(half * HG, (half + 1) * HG):
                        conv(hq, i, first and i < NCV)
                    if tables:
                        k_group(2 * hq + half + 2)

            k_group(0)
            k_group(1)
            pe.wait_ge(s_xt0, 16)
            sixteen(0, first=True)
            pe.wait_ge(s_xt, 16 * (HQ - 1))
            with pe.Fori(1, HQ - 1) as hq:
                sixteen(hq)
            sixteen(HQ - 1, tables=False)

            def mm(out, w, x, start, stop):
                return nc.tensor.matmul(out, w, x, start=start, stop=stop, skip_group_check=True)

            def tile(w, slot, k, rows=P):
                return w[0:rows, slot, k * P:(k + 1) * P]

            def passes(out, slot, k, hi, lo, start, stop, rows=P):
                mm(out, tile(whi, slot, k, rows), hi, start, False)
                mm(out, tile(whi, slot, k, rows), lo, False, False)
                return mm(out, tile(wlo, slot, k, rows), hi, False, stop)

            def x_tiles(bank, slot):
                for k in range(C):
                    passes(ps[bank][:, :], slot, k, xhi[:, k, :], xlo[:, k, :], k == 0, False)

            def sweep(j):
                n0 = UNITS * j
                for g in range(2):
                    pe.wait_ge(s_wlo, n0 + g + 1)
                    for k in range(C):
                        if g == 0:
                            pe.wait_ge(s_xlo, C * j + k + 1)
                        last = passes(of_group(ps[0][:, :], g), g, k, of_group(xhi[:, k, :], g),
                                      of_group(xlo[:, k, :], g), k == 0, k == C - 1)
                    last.then_inc(s_unit, 1)
                pe.wait_ge(s_wlo, n0 + 3)
                x_tiles(2, 2)
                pe.wait_ge(s_t, j + 1)
                for g in range(2):
                    last = passes(of_group(ps[2][:, :], g), 2, C + g, of_group(thi[:, :], g),
                                  of_group(tlo[:, :], g), False, True)
                last.then_inc(s_unit, 1)
                pe.wait_ge(s_tz, 1)
                with pe.Fori(0, FT // 3) as t:
                    for q in range(6):
                        bank, slot, half = (GU0 + q) % 6, q % NSLOT, q % 2
                        pe.wait_ge(s_wlo, n0 + GU0 + 6 * t + q + 1)
                        if half == 0:
                            pe.wait_ge(s_ev, EVS * j + EV_GU + 3 * t + q // 2 - 1)
                        x_tiles(bank, slot)
                        if q == 0:
                            pe.wait_ge(s_tsa, 2 * (j + 1))
                            pe.wait_ge(s_tsd, 4 * (j + 1))
                        for g in range(2):
                            out = of_group(ps[bank][:, :], g)
                            mm(out, tile(whi, slot, C + g), of_group(ts[:, half, :], g), False, False)
                            last = mm(out, tile(wlo, slot, C + g), of_group(tz[:, half, :], g), False, True)
                        last.then_inc(s_unit, 1)
                k0 = 0
                for u, kt in enumerate(TDT):
                    pe.wait_ge(s_wlo, n0 + TD0 + u + 1)
                    pe.wait_ge(s_tdl, 3 * j + u + 1)
                    pe.wait_ge(s_act, ACS * j + min(k0 + kt + 1, ACS))
                    for k in range(kt):
                        kk = k0 + k
                        rows, at = (P, kk + 1) if kk < FT else (FR, 0)
                        for g, w in enumerate((whi, wlo)):
                            out = of_group(ps[6][:, :], g)
                            for half in range(2):
                                last = mm(out, tile(w, u, k, rows), of_group(acts[0:rows, at, half, :], g),
                                          kk == 0 and g == 0 and half == 0, kk == FT and half == 1)
                    last.then_inc(s_unit, 1)
                    k0 += kt

                def output(c, bank):
                    for u, kt in enumerate(DNT):
                        pe.wait_ge(s_wlo, n0 + DN0 + 3 * c + u + 1)
                        if u == 0:
                            pe.wait_ge(s_ev, EVS * j + EV_Y + c - 1)
                        for k in range(min(kt, FT - 8 * u)):
                            at = 8 * u + k + 1
                            last = passes(ps[bank][:, :], u, k, acts[:, at, 0, :], acts[:, at, 1, :],
                                          u + k == 0, False)
                        if u == 2:
                            pe.wait_ge(s_td, j + 1)
                            for g in range(2):
                                last = passes(of_group(ps[bank][:, :], g), u, 5 + g,
                                              of_group(acts[:, 0, 0, :], g), of_group(acts[:, 0, 1, :], g),
                                              False, True)
                        last.then_inc(s_unit, 1)

                with pe.Fori(0, C // 2) as c2:
                    output(2 * c2, 7)
                    output(2 * c2 + 1, 6)

            with pe.Fori(0, SW) as j:
                sweep(j)

        @block.scalar
        def _(act):
            def function(out, in_, func, **kw):
                return nc.scalar.activation(out, in_, func, **kw)

            def copy(out, in_):
                return nc.scalar.activation(out, in_, ACT.Copy)

            act.wait_ge(s_small, 1)
            function(sm["trig"][:, :], sm["ang"][:, :], ACT.Sin, scale=SIN_SCALE).then_inc(s_smallA, 1)

            def tables(g):
                act.wait_ge(s_arg, 2 * g + 1)
                function(tb["m"][:], tb["q"][:], ACT.Exp).then_inc(s_trig, 1)
                act.wait_ge(s_arg, 2 * g + 2)
                function(tb["tr"][:], tb["f3"][:], ACT.Sin, scale=SIN_SCALE).then_inc(s_trig, 1)
                function(th["s1"][:], tb["f"][:, :, 0:NA], ACT.Sin, scale=SIN_SCALE).then_inc(s_trig, 1)
                act.wait_ge(s_ksb, g + 1)
                dst = k_ap[bass.ds(HG * g, HG), P:KPAD].rearrange("h (a b) -> a h b", b=NA)
                act.dma_start(dst, ksb[0:NA, :, :]).then_inc(s_kst, 16)

            with act.Fori(0, NG) as g:
                tables(g)

            def split_hi(j, m, t=0, first=False):
                slot, w = m % NSLOT, tiles_of(m)
                act.wait_ge(s_raw[slot], LOADS * j + loads_of(m) + 96 * t)
                if not first:
                    act.wait_ge(s_unit, UNITS * j + m + 6 * t - NSLOT + 1)
                if TD0 <= m < DN0:
                    for g, (out, s) in enumerate(((whi, s_tdh), (wlo, s_whi))):
                        copy(out[:, slot, 0:w * P].rearrange("p (k n) -> p k n", n=P)[:, :, 0:FR],
                             raw[:, slot, 0:w * P].rearrange("p (k g n) -> p k g n", g=2, n=FR)[:, :, g, :]
                             ).then_inc(s, 1)
                else:
                    copy(whi[:, slot, 0:w * P], raw[:, slot, 0:w * P]).then_inc(s_whi, 1)

            def chunk_in(j, c):
                act.dma_start(xns[:, c % 2, :], xn_d[:, j, c, :]).then_inc(s_xn[c % 2], 16)
                if not (isinstance(j, int) and j == 0):
                    act.dma_start(y1s[:, c % 2, :].rearrange("p (q n) -> p q n", q=HQ), y1_d[:, j, :, c, :]).then_inc(s_y1[c % 2], 16)

            def x_hi(j, c):
                act.wait_ge(s_xsum, C * j + c + 1)
                copy(xhi[:, c, :], y1s[:, c % 2, :]).then_inc(s_xhi, 1)
                act.dma_start(x1_d[:, j, c, :], y1s[:, c % 2, :]).then_inc(s_x1st[c % 2], 16)

            def chunk_free(j, c):
                act.wait_ge(s_xlo, C * j + c + 1)
                act.wait_ge(s_x1st[c % 2], 16 * (C // 2) * j + 16 * (c // 2 + 1))

            def residual_in(j, c):
                if c < 2:
                    act.wait_ge(s_x1st[c % 2], 16 * (C // 2) * (j + 1))
                else:
                    act.wait_ge(s_out[c % 2], 16 * (C // 2) * j + 16 * (c // 2))
                act.dma_start(xres[:, c % 2, :], x1_d[:, j, c, :]).then_inc(s_xres[c % 2], 16)

            def store(j, c):
                act.wait_ge(s_ev, EVS * j + EV_Y + c + 1)
                act.dma_start(out_d[:, j, c, :], xres[:, c % 2, :]).then_inc(s_out[c % 2], 16)

            def act_hi(ev, slot, i3, rows=P):
                act.wait_ge(s_ev, ev + 1)
                copy(acts[0:rows, bass.ds(slot, 1), 0, :].rearrange("p a n -> p (a n)"),
                     sg[0:rows, i3, :]).then_inc(s_hi, 1)

            def steps_gu(j, t, look):
                for q in range(6):
                    m = GU0 + 1 + q
                    look(m + 2, t)
                    act.wait_ge(s_unit, UNITS * j + m + 6 * t)
                    i3, bank = q // 2, (GU0 + q) % 6
                    if q % 2 == 0:
                        function(sg[:, i3, :], ps[bank][:, :], ACT.Silu).then_inc(s_sil, 1)
                    else:
                        act_hi(EVS * j + EV_GU + 3 * t + i3, 3 * t + i3 + 1, i3)

            def sweep(j, last):
                def look(m, t=0):
                    if m < UNITS:
                        split_hi(j, m, t)
                    elif not last:
                        split_hi(j + 1, m - UNITS)

                look(3)
                look(4)
                act.wait_ge(s_ev, EVS * j + EV_T + 1)
                copy(thi[:, :], sg[:, 0, :]).then_inc(s_hi, 1)
                act.wait_ge(s_hi, HIS * j + 1)
                for half in range(2):
                    copy(ts[0:FR, half, :], thi[half * FR:(half + 1) * FR, :].bitcast(F32)).then_inc(s_tsa, 1)
                look(5)
                act.wait_ge(s_unit, UNITS * j + 3)
                function(sg[0:FR, 2, :], ps[2][0:FR, :], ACT.Silu).then_inc(s_sil, 1)
                copy(sg[0:FR, 1, :], ps[2][FR:P, :]).then_inc(s_sil, 1)
                act_hi(EVS * j + EV_L, 0, 2, FR)
                act.wait_ge(s_y1st, 16 * (SW - 1))
                with act.Fori(0, FT // 3 - 1) as t:
                    steps_gu(j, t, look)
                steps_gu(j, FT // 3 - 1, lambda m, t: look(m + 6 * t))
                for m in (48, 49, 50):
                    look(m)
                copy(sg[0:FR, 1, :], ps[6][FR:P, :]).then_inc(s_sil, 1)
                act.wait_ge(s_ev, EVS * j + EV_TD + 2)
                copy(acts[FR:P, 0, 0, :], sg[FR:P, 0, :]).then_inc(s_hi, 1)
                for c in range(2):
                    residual_in(j, c)
                    if not last:
                        chunk_in(j + 1, c)
                for c in range(C):
                    look(DN0 + 3 * c + 3)
                    if c:
                        store(j, c - 1)
                    if not last:
                        x_hi(j + 1, c)
                    look(DN0 + 3 * c + 4)
                    if c and c + 1 < C:
                        residual_in(j, c + 1)
                    if not last and c + 2 < C:
                        chunk_free(j + 1, c)
                        chunk_in(j + 1, c + 2)
                    look(DN0 + 3 * c + 5)
                store(j, C - 1)
                for i in range(2):
                    act.wait_ge(s_out[i], 16 * (C // 2) * (j + 1))

            def conv_out(j):
                act.dma_start(y1_d[:, j].rearrange("p q c n -> p (q c) n"),
                              xt[:, :, :, 2 * j:2 * j + 2, :].rearrange("p q c g n -> p (q c) (g n)")
                              ).then_inc(s_y1st, 16)

            for c in range(2):
                chunk_in(0, c)
            for m in range(NSLOT):
                split_hi(0, m, first=True)
            act.wait_ge(s_cev, H)
            for c in range(C):
                x_hi(0, c)
                if c + 2 < C:
                    chunk_free(0, c)
                    chunk_in(0, c + 2)
            for j in range(1, SW):
                conv_out(j)
            with act.Fori(0, SW - 1) as j:
                sweep(j, False)
            sweep(SW - 1, True)

        @block.vector
        def _(dve):
            V = nc.vector
            count = [0]

            def step(ins):
                count[0] += 1
                ins.then_inc(s_chain, 1)
                return count[0]

            def after(n):
                dve.wait_ge(s_chain, n)

            def link(ins):
                after(step(ins))

            def together(*chains):
                last = {c: 0 for c in chains}
                while last:
                    for c in list(last):
                        if last[c]:
                            after(last[c])
                        last[c] = next(c, None)
                        if last[c] is None:
                            del last[c]
                after(count[0])

            def exp(dst, z, k, r, p, bits):
                yield step(V.tensor_scalar(p, z, 88.0, -87.0, ALU.min, ALU.max))
                yield step(V.tensor_scalar(k, p, 1.4426950408889634, MAGIC, ALU.mult, ALU.add))
                yield step(V.tensor_scalar(k, k, MAGIC, None, ALU.subtract))
                yield step(V.scalar_tensor_tensor(r, k, -LN_A, p, ALU.mult, ALU.add))
                yield step(V.scalar_tensor_tensor(r, k, -LN_B, r, ALU.mult, ALU.add))
                yield step(V.tensor_scalar(bits, k, 127.0, 8388608.0, ALU.add, ALU.mult))
                yield step(V.tensor_scalar(p, r, 1.0 / 5040, None, ALU.mult))
                for f in (720, 120, 24, 6, 2, 1):
                    yield step(V.scalar_tensor_tensor(p, p, 1.0 / f, r, ALU.add, ALU.mult))
                yield step(V.scalar_tensor_tensor(dst, p, 1.0, bits.bitcast(F32), ALU.add, ALU.mult))

            dve.wait_ge(s_in, 16 * 3)
            s = {n: sm[n][:] for n in sm}
            dt, are, aim = s["z"][:, 0:H], s["z"][:, H:2 * H], par[:, 2, :]
            together(exp(s["z"], par[:, 0:2, :].rearrange("p a h -> p (a h)"), s["ek"], s["er"], s["ep"], eki[:]))

            def angles():
                kk, v = s["kk"], s["v"]
                yield step(V.tensor_tensor(s["dim"], aim, dt, ALU.mult))
                yield step(V.tensor_scalar(kk, s["dim"], 1.0 / TWO_PI, MAGIC, ALU.mult, ALU.add))
                yield step(V.tensor_scalar(kk, kk, MAGIC, None, ALU.subtract))
                yield step(V.scalar_tensor_tensor(v, kk, -PI_A, s["dim"], ALU.mult, ALU.add))
                yield step(V.scalar_tensor_tensor(v, kk, -PI_B, v, ALU.mult, ALU.add))
                yield step(V.scalar_tensor_tensor(v, kk, -PI_C, v, ALU.mult, ALU.add))
                yield step(V.tensor_scalar(v, v, 1.0 / TWO_PI, None, ALU.mult))
                step(V.tensor_copy(s["ang"][:, 0:H], v))
                yield step(V.tensor_scalar(s["ang"][:, H:2 * H], v, 0.25, None, ALU.add))
                yield step(V.tensor_scalar(s["angk"], s["ang"], MAGIC, MAGIC, ALU.add, ALU.subtract))
                V.tensor_tensor(s["ang"], s["ang"], s["angk"], ALU.subtract).then_inc(s_small, 1)

            def decay():
                yield step(V.scalar_tensor_tensor(s["dre"], are, -1.0, dt, ALU.mult, ALU.mult))
                yield from exp(s["ed"], s["dre"], s["e2k"], s["e2r"], s["e2p"], eki[:, 0:H])

            def quotient():
                cr, ci = par[:, 3, :], par[:, 4, :]
                step(V.tensor_tensor(s["u1"], are, are, ALU.mult))
                yield step(V.tensor_tensor(s["u2"], aim, aim, ALU.mult))
                yield step(V.tensor_tensor(s["rden"], s["u1"], s["u2"], ALU.add))
                step(V.reciprocal(s["rden"], s["rden"]))
                step(V.tensor_tensor(s["u1"], cr, are, ALU.mult))
                step(V.tensor_tensor(s["u2"], ci, aim, ALU.mult))
                step(V.tensor_tensor(s["u3"], ci, are, ALU.mult))
                yield step(V.tensor_tensor(s["u4"], cr, aim, ALU.mult))
                step(V.tensor_tensor(s["qr"], s["u2"], s["u1"], ALU.subtract))
                yield step(V.scalar_tensor_tensor(s["qi"], s["u3"], -1.0, s["u4"], ALU.mult, ALU.subtract))
                step(V.tensor_tensor(s["qr"], s["qr"], s["rden"], ALU.mult))
                yield step(V.tensor_tensor(s["qi"], s["qi"], s["rden"], ALU.mult))

            together(angles(), decay(), quotient())

            def over_steps(x, g, w):
                return x[:, bass.ds(HG * g, HG)].unsqueeze(2).broadcast_to([P, HG, w])

            def over_heads(col):
                return cst[:, col:col + 2 * NA].unsqueeze(1).broadcast_to([P, HG, 2 * NA])

            STEPS = 9
            t = {n: tb[n][:] for n in tb} | {n: th[n][:] for n in th}

            class Group:
                def __init__(self, g, base):
                    self.g, self.base, self.n = g, base, 0

                def link(self, ins):
                    ins.then_inc(s_chain, 1)
                    self.n += 1
                    dve.wait_ge(s_chain, self.base + STEPS * self.g + self.n)

            def arguments(grp):
                g = grp.g
                V.tensor_tensor(t["q"], over_steps(s["dre"], g, 2 * NA), over_heads(CAB), ALU.mult).then_inc(s_arg, 1)
                grp.link(V.tensor_tensor(t["p"], over_steps(s["v"], g, 2 * NA), over_heads(CAB), ALU.mult))
                grp.link(V.tensor_scalar(t["k"], t["p"], MAGIC, MAGIC, ALU.add, ALU.subtract))
                grp.link(V.tensor_tensor(t["f"], t["p"], t["k"], ALU.subtract))
                grp.link(V.tensor_tensor(t["g"], t["f"], over_heads(CPH), ALU.add))
                grp.link(V.tensor_scalar(t["k"], t["g"], MAGIC, MAGIC, ALU.add, ALU.subtract))
                V.tensor_tensor(t["f3"], t["g"], t["k"], ALU.subtract).then_inc(s_arg, 1)

            def products(grp, wait_prev):
                g = grp.g
                dve.wait_ge(s_trig, 3 * g + 3)
                V.tensor_tensor(t["t1"], t["tr"][:, :, 0:NA], over_steps(s["c1"], g, NA), ALU.mult).then_inc(s_chain, 1)
                grp.n += 1
                grp.link(V.tensor_tensor(t["t2"], t["s1"], over_steps(s["c2"], g, NA), ALU.mult))
                grp.link(V.tensor_tensor(t["t1"], t["t1"], t["t2"], ALU.add))
                if wait_prev:
                    dve.wait_ge(s_kmm, g)
                V.tensor_tensor(t["gg"], t["t1"], t["m"][:, :, 0:NA], ALU.mult)
                V.tensor_tensor(t["e2"], t["tr"][:, :, NA:2 * NA], t["m"][:, :, NA:2 * NA], ALU.mult).then_inc(s_tab, 1)

            def k_out(grp, wait_store):
                g = grp.g
                dve.wait_ge(s_kmm, g + 1)
                if wait_store:
                    dve.wait_ge(s_kst, 16 * g)
                grp.link(V.tensor_copy(ksb[0:NA, :, :].rearrange("p h b -> p (h b)"), ps[7][0:NA, 0:HG * NA]))
                assert grp.n == STEPS
                dst = ksb[0:1, :, 0:1].rearrange("p h b -> p (h b)")
                V.tensor_tensor(dst, dst, par[0:1, 5, bass.ds(HG * g, HG)], ALU.add).then_inc(s_ksb, 1)

            COEF = 13
            first = Group(0, count[0])
            arguments(first)
            count[0] += first.n
            c0 = count[0]
            dve.wait_ge(s_smallA, 1)
            sn, cs = s["trig"][:, 0:H], s["trig"][:, H:2 * H]
            step(V.tensor_tensor(s["ei"], s["ed"], sn, ALU.mult))
            link(V.tensor_tensor(s["er1"], s["ed"], cs, ALU.mult))
            link(V.tensor_scalar(s["er1"], s["er1"], 1.0, None, ALU.subtract))
            step(V.tensor_tensor(s["u1"], s["qr"], s["er1"], ALU.mult))
            step(V.tensor_tensor(s["u2"], s["qi"], s["ei"], ALU.mult))
            step(V.tensor_tensor(s["u3"], s["qr"], s["ei"], ALU.mult))
            link(V.tensor_tensor(s["u4"], s["qi"], s["er1"], ALU.mult))
            step(V.tensor_tensor(s["cr"], s["u1"], s["u2"], ALU.subtract))
            link(V.tensor_tensor(s["ci"], s["u3"], s["u4"], ALU.add))
            al, be, nal = (cst[:, x:x + 1] for x in (CAL, CBE, CNAL))
            step(V.tensor_scalar(s["u1"], s["ci"], be, None, ALU.mult))
            link(V.tensor_scalar(s["u2"], s["cr"], be, None, ALU.mult))
            step(V.scalar_tensor_tensor(s["c1"], s["cr"], al, s["u1"], ALU.mult, ALU.add))
            link(V.scalar_tensor_tensor(s["c2"], s["ci"], nal, s["u2"], ALU.mult, ALU.add))
            assert count[0] - c0 == COEF
            first.base += COEF
            products(first, False)
            V.tensor_copy(lenf[:, :], leni[:, :]).then_inc(s_len, 1)
            dve.wait_ge(s_len, 1)
            for c in range(C):
                V.tensor_scalar(mask[:, c, :], lenf[:, :], cst[:, CPOS + c:CPOS + c + 1], None,
                                ALU.is_gt).then_inc(s_len, 1)
            dve.wait_ge(s_len, 1 + C)
            k_out(first, False)
            base = first.base

            def group(g):
                return Group(g, base)

            grp = group(1)
            arguments(grp)
            products(grp, True)
            k_out(grp, True)

            def evacuate(hq, i):
                dve.wait_ge(s_conv, HH * hq + i + 1)
                out = xt[:, bass.ds(hq, 1), :, :, i * BG:(i + 1) * BG].rearrange("p q c g b -> p (q c) g b")
                V.tensor_tensor(out, ps[i % NCV][:, 0:C * B].rearrange("p (c g b) -> p c g b", c=C, g=G),
                                mask[:].rearrange("p c (g b) -> p c g b", g=G), ALU.mult).then_inc(s_cev, 1)

            with dve.Fori(0, HQ - 1) as hq:
                for half in range(2):
                    grp = group(2 * hq + half + 2)
                    for i in range(half * HG, half * HG + HG // 2):
                        evacuate(hq, i)
                    arguments(grp)
                    for i in range(half * HG + HG // 2, half * HG + 6):
                        evacuate(hq, i)
                    products(grp, True)
                    for i in range(half * HG + 6, (half + 1) * HG):
                        evacuate(hq, i)
                    k_out(grp, True)
            for i in range(HH):
                evacuate(HQ - 1, i)

            def split_lo(j, m, t=0):
                slot, w = m % NSLOT, tiles_of(m)
                dve.wait_ge(s_whi, UNITS * j + m + 6 * t + 1)
                if TD0 <= m < DN0:
                    dve.wait_ge(s_tdh, 3 * j + m - TD0 + 1)
                    for g, (out, sm_) in enumerate(((whi, s_tdl), (wlo, s_wlo))):
                        tiles = out[:, slot, 0:w * P].rearrange("p (k n) -> p k n", n=P)
                        V.tensor_tensor(tiles[:, :, FR:P],
                                        raw[:, slot, 0:w * P].rearrange("p (k g n) -> p k g n", g=2, n=FR)[:, :, g, :],
                                        tiles[:, :, 0:FR].bitcast(F32), ALU.subtract).then_inc(sm_, 1)
                else:
                    V.tensor_tensor(wlo[:, slot, 0:w * P], raw[:, slot, 0:w * P],
                                    whi[:, slot, 0:w * P].bitcast(F32), ALU.subtract).then_inc(s_wlo, 1)

            def x_lo(j, c):
                dve.wait_ge(s_xn[c % 2], 16 * (C // 2) * j + 16 * (c // 2 + 1))
                if isinstance(j, int) and j == 0:
                    as_q = lambda x: x.rearrange("p (q n) -> p q n", q=HQ)
                    V.tensor_tensor(as_q(y1s[:, c % 2, :]),
                                    xt[:, :, c, 0:2, :].rearrange("p q g n -> p q (g n)"),
                                    as_q(xns[:, c % 2, :]), ALU.add).then_inc(s_xsum, 1)
                else:
                    dve.wait_ge(s_y1[c % 2], 16 * (C // 2) * (j - 1) + 16 * (c // 2 + 1))
                    V.tensor_tensor(y1s[:, c % 2, :], y1s[:, c % 2, :], xns[:, c % 2, :], ALU.add).then_inc(s_xsum, 1)
                dve.wait_ge(s_xhi, C * j + c + 1)
                V.tensor_tensor(xlo[:, c, :], y1s[:, c % 2, :], xhi[:, c, :].bitcast(F32),
                                ALU.subtract).then_inc(s_xlo, 1)

            def by_batch(x):
                return x.rearrange("p (n b) -> p n b", b=BG)

            def lora_mask(rows):
                return cst[rows, CMASK:CMASK + BG].unsqueeze(1).broadcast_to([rows.stop - rows.start, T // BG, BG])

            def act_lo(hi_count, slot, i3, rows=P):
                dve.wait_ge(s_hi, hi_count)
                tile = acts[0:rows, bass.ds(slot, 1), :, :].rearrange("p a h n -> p (a h) n")
                V.tensor_tensor(tile[:, 1, :], sg[0:rows, i3, :], tile[:, 0, :].bitcast(F32),
                                ALU.subtract).then_inc(s_act, 1)

            def steps_gu(j, t_, look):
                for q in range(6):
                    m = GU0 + 1 + q
                    look(m + 2, t_)
                    if q % 2:
                        i3, bank = q // 2, (GU0 + q) % 6
                        dve.wait_ge(s_unit, UNITS * j + m + 6 * t_)
                        dve.wait_ge(s_sil, SIL * j + 2 + 3 * t_ + i3 + 1)
                        V.tensor_tensor(sg[:, i3, :], sg[:, i3, :], ps[bank][:, :], ALU.mult).then_inc(s_ev, 1)
                        act_lo(HIS * j + 2 + 3 * t_ + i3 + 1, 3 * t_ + i3 + 1, i3)

            def sweep(j, last):
                def look(m, t_=0):
                    if m < UNITS:
                        split_lo(j, m, t_)
                    elif not last:
                        split_lo(j + 1, m - UNITS)

                look(3)
                look(4)
                dve.wait_ge(s_unit, UNITS * j + 2)
                V.tensor_tensor(by_batch(sg[:, 0, :]), by_batch(ps[0][:, :]), lora_mask(slice(0, P)),
                                ALU.mult).then_inc(s_ev, 1)
                dve.wait_ge(s_hi, HIS * j + 1)
                V.tensor_tensor(tlo[:, :], sg[:, 0, :], thi[:, :].bitcast(F32), ALU.subtract).then_inc(s_t, 1)
                for half in range(2):
                    rows = slice(half * FR, (half + 1) * FR)
                    V.tensor_tensor(ts[FR:P, half, :], sg[rows, 0, :], thi[rows, :].bitcast(F32),
                                    ALU.subtract).then_inc(s_tsd, 1)
                    V.tensor_copy(tz[0:FR, half, :], thi[rows, :].bitcast(F32)).then_inc(s_tsd, 1)
                look(5)
                dve.wait_ge(s_sil, SIL * j + 2)
                V.tensor_tensor(sg[0:FR, 2, :], sg[0:FR, 2, :], sg[0:FR, 1, :], ALU.mult).then_inc(s_ev, 1)
                act_lo(HIS * j + 2, 0, 2, FR)
                with dve.Fori(0, FT // 3 - 1) as t_:
                    steps_gu(j, t_, look)
                steps_gu(j, FT // 3 - 1, lambda m, t_: look(m + 6 * t_))
                for m in (48, 49, 50):
                    look(m)
                dve.wait_ge(s_unit, UNITS * j + DN0)
                dve.wait_ge(s_sil, SIL * (j + 1))
                V.tensor_tensor(sg[0:FR, 1, :], ps[6][0:FR, :], sg[0:FR, 1, :], ALU.add).then_inc(s_ev, 1)
                dve.wait_ge(s_ev, EVS * j + EV_TD + 1)
                V.tensor_tensor(by_batch(sg[FR:P, 0, :]), by_batch(sg[0:FR, 1, :]), lora_mask(slice(0, FR)),
                                ALU.mult).then_inc(s_ev, 1)
                dve.wait_ge(s_hi, HIS * (j + 1))
                V.tensor_tensor(acts[FR:P, 0, 1, :], sg[FR:P, 0, :], acts[FR:P, 0, 0, :].bitcast(F32),
                                ALU.subtract).then_inc(s_td, 1)
                for c in range(C):
                    if not last:
                        x_lo(j + 1, c)
                    for m in range(DN0 + 3 * c + 3, DN0 + 3 * c + 6):
                        look(m)
                    dve.wait_ge(s_unit, UNITS * j + DN0 + 3 * c + 3)
                    dve.wait_ge(s_xres[c % 2], 16 * (C // 2) * j + 16 * (c // 2 + 1))
                    V.tensor_tensor(xres[:, c % 2, :], ps[7 - c % 2][:, :], xres[:, c % 2, :],
                                    ALU.add).then_inc(s_ev, 1)

            dve.wait_ge(s_cev, H)
            for c in range(C):
                if c < NSLOT:
                    split_lo(0, c)
                x_lo(0, c)
            V.memset(tz[FR:P, :, :].bitcast(F32), 0.0).then_inc(s_tz, 1)
            with dve.Fori(0, SW - 1) as j:
                sweep(j, False)
            sweep(SW - 1, True)


def constants():
    p = np.arange(P)
    cst = np.zeros((P, NC_), np.float32)
    cst[:, CAB:CAB + NA] = NA * np.arange(NA)
    cst[:, CAB + NA:CAB + 2 * NA] = np.arange(NA)
    cst[:, CPH:CPH + NA] = 0.25
    cst[:, CPH + NA:CPH + 2 * NA] = np.where(p < NS, 0.25, 0.0)[:, None]
    cst[:, CPOS:CPOS + C] = P * np.arange(C)[None, :] + p[:, None]
    cst[:, CMASK:CMASK + BG] = 0.5 * (p[:, None] // RANK % BG == np.arange(BG)[None, :])
    cst[:, CAL] = np.where(p < NS, 2.0, 0.0)
    cst[:, CBE] = np.where(p < NS, 0.0, -2.0)
    cst[:, CNAL] = -cst[:, CAL]
    return cst


def layouts(x, itok_B_8_3872, itok_B_2_6, L0_cond_log_dt, L0_cond_C, L0_cond_log_A_real, L0_cond_A_imag,
            L0_cond_D, L1_cond_W_gate, L1_cond_W_up, L1_cond_W_down, L1_cond_A_gate, L1_cond_B_gate,
            L1_cond_A_up, L1_cond_B_up, L1_cond_A_down, L1_cond_B_down):
    c = np.ascontiguousarray
    a = {}
    xs = np.asarray(x).reshape(SW, 2, BG, HQ, HH, C, P)
    a["xt"] = c(xs.transpose(6, 3, 5, 0, 1, 4, 2)[::-1].reshape(P, HQ, C, G, HT))
    a["xn"] = c(xs.transpose(6, 0, 5, 3, 1, 4, 2).reshape(P, SW, C, T))
    a["idx"] = c(np.asarray(itok_B_2_6).reshape(1, B))
    a["len"] = c(np.asarray(itok_B_8_3872).reshape(1, B))
    rows = lambda v: np.broadcast_to(np.asarray(v)[None, :], (P, H))
    twice = lambda m: np.concatenate([np.asarray(m).T, np.asarray(m).T], 0)
    Cc = np.asarray(L0_cond_C)
    a["par"] = c(np.stack([rows(L0_cond_log_dt), twice(L0_cond_log_A_real), twice(L0_cond_A_imag),
                           twice(Cc[..., 0]), twice(Cc[..., 1]), rows(L0_cond_D)], 1))
    a["cst"] = constants()
    FW = FT * P
    tiles = lambda w: np.asarray(w)[:FW].reshape(FT, P, C, P).transpose(0, 3, 2, 1).reshape(FT, P, C * P)
    wg, wu = np.asarray(L1_cond_W_gate), np.asarray(L1_cond_W_up)
    a["wgu"] = c(np.concatenate([tiles(wg), tiles(wu)], 2))
    rest = lambda w: w[FW:].reshape(FR, C, P).transpose(2, 1, 0)
    a["wl"] = c(np.concatenate([rest(wg), rest(wu)], 2).reshape(P, C * P))
    bg, bu = (np.asarray(v)[0].transpose(0, 2, 1) for v in (L1_cond_B_gate, L1_cond_B_up))
    a["bgu"] = c(np.stack([v[:, :, :FW].reshape(R, RANK, FT, P).transpose(0, 2, 1, 3) for v in (bg, bu)], 3))
    bl = np.zeros((R, 2, RANK, P), np.float32)
    bl[:, 0, :, 0:FR] = bg[:, :, FW:]
    bl[:, 1, :, FR:P] = bu[:, :, FW:]
    a["bl"] = bl
    wd = np.asarray(L1_cond_W_down)
    a["wd"] = c(wd[:, :FW].reshape(C, P, FT, P).transpose(0, 3, 2, 1).reshape(C, P, FT * P))
    wdl = wd[:, FW:].reshape(C, P, FR).transpose(0, 2, 1)
    a["wdl"] = c(np.stack([wdl, wdl], 2))
    bd = np.asarray(L1_cond_B_down)[0]
    a["bd"] = c(bd.reshape(R, C, P, RANK).transpose(0, 1, 3, 2))
    amat = lambda v: np.asarray(v)[0].reshape(R * RANK, C, P).transpose(2, 1, 0)
    a["agu"] = c(np.stack([amat(L1_cond_A_gate), amat(L1_cond_A_up)], 2).reshape(P, 2 * C, R * RANK))
    ad = np.zeros((P, AK, R * RANK), np.float32)
    v = np.asarray(L1_cond_A_down)[0].reshape(R * RANK, F)
    ad[:, :FT] = v[:, :FW].reshape(R * RANK, FT, P).transpose(2, 1, 0)
    ad[:FR, FT] = v[:, FW:].T
    a["ad"] = ad
    return a


ORDER = ("xt", "xn", "idx", "len", "par", "cst", "wgu", "wl", "bgu", "bl", "wd", "wdl", "bd", "agu", "ad")


def kernel(**inputs):
    import concourse.bacc as bacc
    from concourse.bass_utils import run_bass_kernel_spmd
    arrays = layouts(**inputs)
    nc = bacc.Bacc("TRN2", target_bir_lowering=False, num_devices=1)
    args = [nc.dram_tensor(n, arrays[n].shape, mybir.dt.from_np(arrays[n].dtype), kind="ExternalInput").ap()
            for n in ORDER]
    out = nc.dram_tensor("out", (P, SW, C, T), F32, kind="ExternalOutput").ap()
    build(nc, *args, out)
    r = run_bass_kernel_spmd(nc, [arrays], core_ids=[0])
    y = r.results[0]["out"].reshape(P, SW, C, HQ, 2, HH, BG)
    return np.ascontiguousarray(y.transpose(1, 4, 6, 3, 5, 2, 0)).reshape(B, H, L)
```

```python
from contextlib import ExitStack

import numpy as np
import concourse.bass as bass
from concourse import mybir

F32 = mybir.dt.float32
F32R = mybir.dt.float32r
I32 = mybir.dt.int32
ALU = mybir.AluOpType
ACT = mybir.ActivationFunctionType

P = 128
B, H, L = 32, 64, 1024
F = 2752
R, RANK = 16, 16
C = L // P
G = 8
BG = B // G
SW = 4
T = B * H // SW
FT = F // P
FR = F - FT * P
KT = FT + 1
NS = 64
NA = 32
HQ, HH = 4, 16
HT = HH * BG
KPAD = P + L
HG = 8
NG = H // HG
NTT = 8
NCV = 4

GU0 = 3
TD0 = GU0 + 2 * FT
DN0 = TD0 + 3
UNITS = DN0 + 3 * C
NSLOT = 3
UW = C + 2
assert UNITS % NSLOT == 0 and GU0 % NSLOT == 0 and (2 * FT) % 6 == 0
TDT = (8, 8, 6)
DNT = (8, 8, 7)


def tiles_of(m):
    if m < 2:
        return C
    return UW if m < TD0 else TDT[m - TD0] if m < DN0 else DNT[(m - DN0) % 3]


def loads_of(m):
    if m < GU0:
        return 32
    if m < TD0:
        return 32 + 48 * ((m - GU0) // NSLOT + 1)
    return 32 + 48 * (2 * FT // NSLOT) + 32 * ((m - TD0) // NSLOT + 1)


LOADS = loads_of(UNITS - 1)

EV_T, EV_L, EV_GU, EV_Y = 0, 1, 2, 2 + FT
EVS = EV_Y + C
HIS = 3 + FT
SIL = 3 + FT
GATHERS = 1 + 5 * 8
ACS = 1 + FT

CAB, CPH, CPOS, CMASK, CAL, CBE, CNAL = 0, 64, 128, 136, 140, 141, 142
NC_ = 143

MAGIC = 12582912.0
TWO_PI = 6.283185307179586
PI_A = 6.28125
PI_B = 1014 / 2 ** 19
PI_C = TWO_PI - PI_A - PI_B
LN_A = 0.693359375
LN_B = 0.6931471805599453 - LN_A
SIN_SCALE = float(np.nextafter(np.float32(TWO_PI), np.float32(0)))


def of_group(tile, g):
    return tile.rearrange("p (q g n) -> p q g n", q=HQ, g=2)[:, :, g, :]


def build(nc, xt_d, xn_d, idx_d, len_d, par_d, cst_d, wgu_d, wl_d, bgu_d, bl_d, wd_d, wdl_d, bd_d,
          agu_d, ad_d, out_d):
    def scratch(name, shape):
        return nc.dram_tensor(name, shape, F32, kind="Internal").ap()

    k_d = nc.dram_tensor("k_pad", [H, KPAD], F32, kind="Internal")
    k_ap = k_d.ap()
    y1_d = scratch("conv_out", [P, HQ, C, (SW - 1) * T // HQ])
    x1_d = scratch("x1_keep", [P, SW, C, T])
    bgs_d = scratch("bgu_sel", [SW, FT, FR, 2, 2, P])
    bls_d = scratch("bl_sel", [SW, P, 2, P])
    bds_d = scratch("bd_sel", [SW, C, P, 2, P])
    ags_d = scratch("a_gu_sel", [SW, 2, P, BG, C * 2 * RANK])
    ads_d = scratch("a_down_sel", [SW, P, 2, BG, KT * RANK])

    with ExitStack() as ctx:
        START = (nc.sbuf_base + 31) // 32 * 32
        ARENA = 206 * 1024
        ctx.enter_context(nc.sbuf_tensor("arena", [P, ARENA], mybir.dt.uint8))

        class Region:
            def __init__(self, start):
                self.at = start

            def take(self, name, shape, dt=F32):
                t = nc.alloc_sbuf_tensor_at(name, [P, *shape], dt, offset=self.at)
                self.at += (int(np.prod(shape)) * 4 + 31) // 32 * 32
                assert self.at <= START + ARENA, (name, self.at - START)
                return t

        common = Region(START)
        raw = common.take("raw", [NSLOT, UW * P])
        whi = common.take("whi", [NSLOT, UW * P], F32R)
        cst = common.take("cst", [NC_])
        idx = common.take("idx", [B], I32)
        xn0 = nc.alloc_sbuf_tensor_at("xn0", [P, HQ, C, T // HQ], F32, offset=common.at)
        wlo = common.take("wlo", [NSLOT, UW * P], F32R)
        y1s = common.take("y1s", [2, T])
        xns = common.take("xns", [2, T])
        ACT_FIRST = 6
        a = Region(common.at)
        par = a.take("par", [6, H])
        leni = a.take("leni", [B], I32)
        lenf = a.take("lenf", [B])
        mask = a.take("mask", [C, B])
        zero = a.take("zero", [P])
        eki = a.take("eki", [2 * H], I32)
        wide = ("z", "ek", "er", "ep", "ang", "angk", "trig")
        sm = {n: a.take("sm_" + n, [2 * H if n in wide else H]) for n in wide + (
            "dre", "dim", "v", "kk", "ed", "e2k", "e2r", "e2p", "er1", "ei", "qr", "qi",
            "u1", "u2", "u3", "u4", "rden", "cr", "ci", "c1", "c2")}
        assert a.at <= common.at + ACT_FIRST * 2 * T * 4
        a.at = common.at + ACT_FIRST * 2 * T * 4
        xt = a.take("xt", [HQ, C, G, HT])
        tt = a.take("tt", [NTT, L])
        tb = {n: a.take("tb_" + n, [HG, 2 * NA]) for n in ("p", "k", "f", "g", "f3", "q", "m", "tr")}
        th = {n: a.take("th_" + n, [HG, NA]) for n in ("s1", "t1", "t2", "gg", "e2")}
        ksb = a.take("ksb", [HG, NA])
        b = Region(common.at)
        acts = b.take("acts", [KT, 2, T], F32R)
        xhi = b.take("xhi", [C, T], F32R)
        xlo = b.take("xlo", [C, T], F32R)
        thi = b.take("thi", [T], F32R)
        tlo = b.take("tlo", [T], F32R)
        ts = b.take("ts", [2, T], F32R)
        tz = b.take("tz", [2, T], F32R)
        sg = b.take("sg", [3, T])
        xres = b.take("xres", [2, T])

        ps = [ctx.enter_context(nc.psum_tensor(f"ps{i}", [P, 512], F32)) for i in range(8)]

        def sem(name):
            return ctx.enter_context(nc.semaphore(name))

        s_in = sem("s_in")
        s_idx = sem("s_idx")
        s_xt0 = sem("s_xt0")
        s_xt = sem("s_xt")
        s_zero = sem("s_zero")
        s_zst = sem("s_zst")
        s_chain = sem("s_chain")
        s_len = sem("s_len")
        s_tz = sem("s_tz")
        s_small = sem("s_small")
        s_smallA = sem("s_smallA")
        s_arg = sem("s_arg")
        s_trig = sem("s_trig")
        s_tab = sem("s_tab")
        s_kmm = sem("s_kmm")
        s_ksb = sem("s_ksb")
        s_kst = sem("s_kst")
        s_tt = [sem(f"s_tt{i}") for i in range(NTT)]
        s_conv = sem("s_conv")
        s_cev = sem("s_cev")
        s_y1st = sem("s_y1st")
        s_gat = sem("s_gat")
        s_raw = [sem(f"s_raw{i}") for i in range(NSLOT)]
        s_whi = sem("s_whi")
        s_wlo = sem("s_wlo")
        s_tdh = sem("s_tdh")
        s_tdl = sem("s_tdl")
        s_unit = sem("s_unit")
        s_ev = sem("s_ev")
        s_hi = sem("s_hi")
        s_sil = sem("s_sil")
        s_t = sem("s_t")
        s_tsa = sem("s_tsa")
        s_tsd = sem("s_tsd")
        s_tde = sem("s_tde")
        s_td = sem("s_td")
        s_act = sem("s_act")
        s_y1 = [sem(f"s_y1{i}") for i in range(2)]
        s_xn = [sem(f"s_xn{i}") for i in range(2)]
        s_x0 = sem("s_x0")
        s_x1 = sem("s_x1")
        s_xsum = sem("s_xsum")
        s_xhi = sem("s_xhi")
        s_xlo = sem("s_xlo")
        s_x1st = [sem(f"s_x1st{i}") for i in range(2)]
        s_xres = [sem(f"s_xres{i}") for i in range(2)]
        s_out = [sem(f"s_out{i}") for i in range(2)]

        def gate_up_tiles(x, slot):
            return x[:, slot, 0:C * P].rearrange("p (kw b r) -> p kw b r", b=BG, r=RANK)

        def gate_up_raw(slot):
            return raw[:, slot, 0:C * P].rearrange("p (b kw r) -> p kw b r", b=BG, r=RANK)

        def down_rows(x, slot, w, at):
            return x[:, slot, 0:w * P].rearrange("p (k n) -> p k n", n=P)[:, :, at:at + FR].rearrange(
                "p k (b r) -> p k b r", b=BG)

        def down_raw(slot, w, g):
            return raw[:, slot, g * w * FR:(g + 1) * w * FR].rearrange("p (b k r) -> p k b r", b=BG, r=RANK)

        def conv_out(engine, q):
            for i in range(2):
                cs = slice(i * C // 2, (i + 1) * C // 2)
                engine.dma_start(y1_d[:, bass.ds(q, 1), cs].rearrange("p q c n -> p (q c) n"),
                                 xt[:, bass.ds(q, 1), cs, 2:G].rearrange("p q c g n -> p (q c) (g n)")
                                 ).then_inc(s_y1st, 16)

        block = ctx.enter_context(nc.Block())

        @block.sync
        def _(sp):
            sp.dma_start(par[:, :, :], par_d).then_inc(s_in, 16)
            sp.dma_start(cst[:, :], cst_d).then_inc(s_in, 16)
            sp.dma_start(idx[0:1, 0:B], idx_d).then_inc(s_idx, 16)
            sp.dma_start(leni[:, :], bass.AP(tensor=len_d.tensor, offset=0, ap=[[0, P], [1, B]])).then_inc(s_in, 16)
            sp.wait_ge(s_zero, 1)
            sp.dma_start(k_ap[:, 0:P], zero[0:H, :]).then_inc(s_zst, 16)
            sp.dma_start(xt[:, 0], xt_d[:, 0]).then_inc(s_xt0, 16)
            sp.dma_start(xt[:, 1], xt_d[:, 1]).then_inc(s_xt, 16)
            sp.wait_ge(s_zst, 16)

            def toeplitz(h, slot):
                src = bass.AP(tensor=k_d, offset=h * KPAD + 1, ap=[[1, P], [1, L]])
                sp.dma_start(tt[:, slot, :], src).then_inc(s_tt[slot], 16)

            sp.wait_ge(s_kst, 16)
            for h in range(HG):
                toeplitz(h, h)

            def xt_half(q, i):
                cs = slice(i * C // 2, (i + 1) * C // 2)
                sp.dma_start(xt[:, q, cs], xt_d[:, q, cs]).then_inc(s_xt, 16)

            def toeplitz_group(g, between=()):
                sp.wait_ge(s_kst, 16 * (g + 1))
                for i in range(HG):
                    sp.wait_ge(s_conv, HG * (g - 1) + i + 1)
                    toeplitz(HG * g + i, i)
                    if i in between:
                        xt_half(*between[i])

            xt_half(2, 0)
            toeplitz_group(1, {1: (2, 1), 4: (3, 0), 7: (3, 1)})

            def x_rows(q):
                src = xn_d[:, 0].rearrange("p c (q n) -> p q c n", q=HQ)[:, bass.ds(q, 1)]
                sp.dma_start(xn0[:, bass.ds(q, 1)].rearrange("p q c n -> p (q c) n"),
                             src.rearrange("p q c n -> p (q c) n")).then_inc(s_x0, 16)

            x_rows(0)
            with sp.Fori(1, HQ) as q:
                toeplitz_group(2 * q)
                x_rows(q)
                toeplitz_group(2 * q + 1)
                sp.wait_ge(s_cev, HH * q)
                conv_out(sp, q - 1)

            def load(m, n, *parts):
                slot = m % NSLOT
                if n is not None:
                    sp.wait_ge(s_wlo, n - NSLOT + 1)
                for rows, t0, t1, src in parts:
                    dst = raw[rows[0]:rows[1], slot, t0 * P:t1 * P]
                    if len(src.shape) == 3:
                        dst = dst.rearrange("p (a n) -> p a n", a=src.shape[1])
                    sp.dma_start(dst, src).then_inc(s_raw[slot], 16)

            ALL = (0, P)

            def flat(x):
                return x.rearrange("p a n -> p (a n)")

            def head_units(j, n0):
                sp.wait_ge(s_gat, 16 * GATHERS * (j + 1))
                for g in range(2):
                    load(g, None if n0 is None else n0 + g, (ALL, 0, 4, flat(ags_d[j, g, :, 0:2])),
                         (ALL, 4, 8, flat(ags_d[j, g, :, 2:4])))
                load(2, None if n0 is None else n0 + 2, (ALL, 0, 8, wl_d), (ALL, 8, 10, flat(bls_d[j])))

            def body_units(j):
                n0 = UNITS * j
                with sp.Fori(0, FT // 3) as t:
                    for q in range(6):
                        i, half = 3 * t + q // 2, q % 2
                        sel = flat(bgs_d[j, i, :, half])
                        load(GU0 + q, n0 + GU0 + 6 * t + q,
                             (ALL, 0, 8, wgu_d[i, :, half * C * P:(half + 1) * C * P]),
                             ((0, FR), 8, 10, sel), ((FR, P), 8, 10, sel))
                k0 = 0
                for u, k in enumerate(TDT):
                    load(TD0 + u, n0 + TD0 + u, *((ALL, g * k // 2, (g + 1) * k // 2,
                                                   ads_d[j, :, g, :, k0 * RANK:(k0 + k) * RANK]) for g in range(2)))
                    k0 += k
                with sp.Fori(0, C) as c:
                    n = n0 + DN0 + 3 * c
                    for u in range(2):
                        load(DN0 + u, n + u, *((ALL, 4 * v, 4 * v + 4,
                                                wd_d[c, :, (8 * u + 4 * v) * P:(8 * u + 4 * v + 4) * P])
                                               for v in range(2)))
                    load(DN0 + 2, n + 2, (ALL, 0, 5, wd_d[c, :, 16 * P:21 * P]), (ALL, 5, 7, flat(bds_d[j, c])))

            head_units(0, None)
            with sp.Fori(0, SW - 1) as j:
                body_units(j)
                head_units(j + 1, UNITS * (j + 1))
            body_units(SW - 1)

        @block.gpsimd
        def _(pool):
            pool.memset(zero[:, :], 0.0).then_inc(s_zero, 1)
            pool.wait_ge(s_idx, 16)

            def adapter(j, b8):
                return pool.value_load(idx[0:1, bass.ds(8 * j + b8, 1)], min_val=0, max_val=R - 1)

            def gather(j):
                pool.dma_start(bds_d[j, :, 0:FR, :, :], wdl_d).then_inc(s_gat, 16)
                for b8 in range(8):
                    r, g, b, r0 = adapter(j, b8), b8 // BG, b8 % BG, (b8 % BG) * RANK
                    pool.dma_start(ags_d[j, g, :, b, :], agu_d[r]).then_inc(s_gat, 16)
                    pool.dma_start(bls_d[j].rearrange("(w p) g n -> w p g n", w=2)[:, r0:r0 + RANK, g, :],
                                   bl_d[r]).then_inc(s_gat, 16)
                    pool.dma_start(bgs_d[j, :, r0:r0 + RANK, :, g, :], bgu_d[r]).then_inc(s_gat, 16)
                    pool.dma_start(ads_d[j, :, g, b, :], ad_d[r]).then_inc(s_gat, 16)
                    pool.dma_start(bds_d[j, :, FR + r0:FR + r0 + RANK, g, :], bd_d[r]).then_inc(s_gat, 16)

            gather(0)
            pool.wait_ge(s_cev, H)
            with pool.Fori(1, SW) as j:
                pool.wait_ge(s_gat, 16 * GATHERS * j)
                pool.wait_ge(s_idx, 16)
                gather(j)

        @block.tensor
        def _(pe):
            def k_group(g):
                pe.wait_ge(s_tab, g + 1)
                for i in range(HG):
                    last = nc.tensor.matmul(ps[7][0:NA, i * NA:(i + 1) * NA], th["gg"][:, i, :],
                                            th["e2"][:, i, :], start=True, stop=True)
                last.then_inc(s_kmm, 1)

            def conv(hq, i, first=False):
                slot, bank = i % NTT, i % NCV
                pe.wait_ge(s_tt[slot], 16 * (2 * hq + i // NTT + 1))
                if not first:
                    pe.wait_ge(s_cev, HH * hq + i - NCV + 1)
                for d in range(C):
                    mov = xt[:, bass.ds(hq, 1), 0:C - d, :, i * BG:(i + 1) * BG].rearrange(
                        "p q c g b -> p (q c) g b")
                    last = nc.tensor.matmul(ps[bank][:, d * B:C * B], tt[:, slot, d * P:(d + 1) * P], mov,
                                            start=(d == 0), stop=(d == C - 1), skip_group_check=True)
                last.then_inc(s_conv, 1)

            def sixteen(hq, first=False, tables=True):
                for half in range(2):
                    for i in range(half * HG, (half + 1) * HG):
                        conv(hq, i, first and i < NCV)
                        if first and i == 1:
                            k_group(1)
                    if tables:
                        k_group(2 * hq + half + 2)

            k_group(0)
            pe.wait_ge(s_xt0, 16)
            sixteen(0, first=True)
            pe.wait_ge(s_xt, 16 * (1 + 4))
            with pe.Fori(1, HQ - 1) as hq:
                sixteen(hq)
            sixteen(HQ - 1, tables=False)

            def mm(out, w, x, start, stop):
                return nc.tensor.matmul(out, w, x, start=start, stop=stop, skip_group_check=True)

            def tile(w, slot, k, rows=P):
                return w[0:rows, slot, k * P:(k + 1) * P]

            def passes(out, slot, k, hi, lo, start, stop, rows=P):
                mm(out, tile(whi, slot, k, rows), hi, start, False)
                mm(out, tile(whi, slot, k, rows), lo, False, False)
                return mm(out, tile(wlo, slot, k, rows), hi, False, stop)

            def x_tiles(bank, slot):
                for k in range(C):
                    passes(ps[bank][:, :], slot, k, xhi[:, k, :], xlo[:, k, :], k == 0, False)

            def sweep(j):
                n0 = UNITS * j
                for g in range(2):
                    pe.wait_ge(s_wlo, n0 + g + 1)
                    for k in range(C):
                        if g == 0:
                            pe.wait_ge(s_xlo, C * j + k + 1)
                        last = passes(of_group(ps[0][:, :], g), g, k, of_group(xhi[:, k, :], g),
                                      of_group(xlo[:, k, :], g), k == 0, k == C - 1)
                    last.then_inc(s_unit, 1)
                pe.wait_ge(s_wlo, n0 + 3)
                x_tiles(2, 2)
                pe.wait_ge(s_t, j + 1)
                for g in range(2):
                    last = passes(of_group(ps[2][:, :], g), 2, C + g, of_group(thi[:, :], g),
                                  of_group(tlo[:, :], g), False, True)
                last.then_inc(s_unit, 1)
                pe.wait_ge(s_tz, 1)
                with pe.Fori(0, FT // 3) as t:
                    for q in range(6):
                        bank, slot, half = (GU0 + q) % 6, q % NSLOT, q % 2
                        pe.wait_ge(s_wlo, n0 + GU0 + 6 * t + q + 1)
                        if half == 0:
                            pe.wait_ge(s_ev, EVS * j + EV_GU + 3 * t + q // 2 - 1)
                        x_tiles(bank, slot)
                        if q == 0:
                            pe.wait_ge(s_tsa, 2 * (j + 1))
                            pe.wait_ge(s_tsd, 4 * (j + 1))
                        for g in range(2):
                            out = of_group(ps[bank][:, :], g)
                            mm(out, tile(whi, slot, C + g), of_group(ts[:, half, :], g), False, False)
                            last = mm(out, tile(wlo, slot, C + g), of_group(tz[:, half, :], g), False, True)
                        last.then_inc(s_unit, 1)
                k0 = 0
                for u, kt in enumerate(TDT):
                    pe.wait_ge(s_wlo, n0 + TD0 + u + 1)
                    pe.wait_ge(s_tdl, 3 * j + u + 1)
                    pe.wait_ge(s_act, ACS * j + min(k0 + kt + 1, ACS))
                    for k in range(kt):
                        kk = k0 + k
                        rows, at = (P, kk + 1) if kk < FT else (FR, 0)
                        for g, w in enumerate((whi, wlo)):
                            out = of_group(ps[6][:, :], g)
                            for half in range(2):
                                last = mm(out, tile(w, u, k, rows), of_group(acts[0:rows, at, half, :], g),
                                          kk == 0 and g == 0 and half == 0, kk == FT and half == 1)
                    last.then_inc(s_unit, 1)
                    k0 += kt

                def output(c, bank):
                    for u, kt in enumerate(DNT):
                        pe.wait_ge(s_wlo, n0 + DN0 + 3 * c + u + 1)
                        if u == 0:
                            pe.wait_ge(s_ev, EVS * j + EV_Y + c - 1)
                        for k in range(min(kt, FT - 8 * u)):
                            at = 8 * u + k + 1
                            last = passes(ps[bank][:, :], u, k, acts[:, at, 0, :], acts[:, at, 1, :],
                                          u + k == 0, False)
                        if u == 2:
                            pe.wait_ge(s_td, j + 1)
                            for g in range(2):
                                last = passes(of_group(ps[bank][:, :], g), u, 5 + g,
                                              of_group(acts[:, 0, 0, :], g), of_group(acts[:, 0, 1, :], g),
                                              False, True)
                        last.then_inc(s_unit, 1)

                with pe.Fori(0, C // 2) as c2:
                    output(2 * c2, 7)
                    output(2 * c2 + 1, 6)

            with pe.Fori(0, SW) as j:
                sweep(j)

        @block.scalar
        def _(act):
            def function(out, in_, func, **kw):
                return nc.scalar.activation(out, in_, func, **kw)

            def copy(out, in_):
                return nc.scalar.activation(out, in_, ACT.Copy)

            act.wait_ge(s_small, 1)
            function(sm["trig"][:, :], sm["ang"][:, :], ACT.Sin, scale=SIN_SCALE).then_inc(s_smallA, 1)

            def tables(g):
                act.wait_ge(s_arg, 2 * g + 1)
                function(tb["m"][:], tb["q"][:], ACT.Exp).then_inc(s_trig, 1)
                act.wait_ge(s_arg, 2 * g + 2)
                function(tb["tr"][:], tb["f3"][:], ACT.Sin, scale=SIN_SCALE).then_inc(s_trig, 1)
                function(th["s1"][:], tb["f"][:, :, 0:NA], ACT.Sin, scale=SIN_SCALE).then_inc(s_trig, 1)
                act.wait_ge(s_ksb, g + 1)
                dst = k_ap[bass.ds(HG * g, HG), P:KPAD].rearrange("h (a b) -> a h b", b=NA)
                act.dma_start(dst, ksb[0:NA, :, :]).then_inc(s_kst, 16)

            with act.Fori(0, NG) as g:
                tables(g)

            def split_hi(j, m, t=0, first=False):
                slot, w = m % NSLOT, tiles_of(m)
                act.wait_ge(s_raw[slot], LOADS * j + loads_of(m) + 96 * t)
                if not first:
                    act.wait_ge(s_unit, UNITS * j + m + 6 * t - NSLOT + 1)
                if TD0 <= m < DN0:
                    for g, (out, s) in enumerate(((whi, s_tdh), (wlo, s_whi))):
                        copy(down_rows(out, slot, w, 0), down_raw(slot, w, g)).then_inc(s, 1)
                elif m < 2:
                    copy(gate_up_tiles(whi, slot), gate_up_raw(slot)).then_inc(s_whi, 1)
                else:
                    copy(whi[:, slot, 0:w * P], raw[:, slot, 0:w * P]).then_inc(s_whi, 1)

            def chunk_in(j, c):
                act.dma_start(xns[:, c % 2, :], xn_d[:, j, c, :]).then_inc(s_xn[c % 2], 16)
                act.dma_start(y1s[:, c % 2, :].rearrange("p (q n) -> p q n", q=HQ),
                              y1_d[:, :, c, bass.ds((T // HQ) * (j - 1), T // HQ)]).then_inc(s_y1[c % 2], 16)

            def x_hi(j, c):
                act.wait_ge(s_xsum, C * (j - 1) + c + 1)
                copy(xhi[:, c, :], y1s[:, c % 2, :]).then_inc(s_xhi, 1)
                act.dma_start(x1_d[:, j, c, :], y1s[:, c % 2, :]).then_inc(s_x1st[c % 2], 16)

            def chunk_free(j, c):
                act.wait_ge(s_xlo, C * j + c + 1)
                act.wait_ge(s_x1st[c % 2], 16 * (C // 2) * j + 16 * (c // 2 + 1))

            def residual_in(j, c):
                if c >= 2:
                    act.wait_ge(s_out[c % 2], 16 * (C // 2) * j + 16 * (c // 2))
                act.dma_start(xres[:, c % 2, :], x1_d[:, j, c, :]).then_inc(s_xres[c % 2], 16)

            def store(j, c):
                act.wait_ge(s_ev, EVS * j + EV_Y + c + 1)
                act.dma_start(out_d[:, j, c, :], xres[:, c % 2, :]).then_inc(s_out[c % 2], 16)

            def act_hi(ev, slot, i3, rows=P):
                act.wait_ge(s_ev, ev + 1)
                copy(acts[0:rows, bass.ds(slot, 1), 0, :].rearrange("p a n -> p (a n)"),
                     sg[0:rows, i3, :]).then_inc(s_hi, 1)

            def steps_gu(j, t, look):
                for q in range(6):
                    m = GU0 + 1 + q
                    look(m + 2, t)
                    act.wait_ge(s_unit, UNITS * j + m + 6 * t)
                    i3, bank = q // 2, (GU0 + q) % 6
                    if q % 2 == 0:
                        function(sg[:, i3, :], ps[bank][:, :], ACT.Silu).then_inc(s_sil, 1)
                    else:
                        act_hi(EVS * j + EV_GU + 3 * t + i3, 3 * t + i3 + 1, i3)

            def head(j):
                def look(m):
                    split_hi(j, m)

                look(3)
                act.wait_ge(s_ev, EVS * j + EV_T + 1)
                copy(thi[:, :], sg[:, 0, :]).then_inc(s_hi, 1)
                act.wait_ge(s_hi, HIS * j + 1)
                for half in range(2):
                    copy(ts[0:FR, half, :], thi[half * FR:(half + 1) * FR, :].bitcast(F32)).then_inc(s_tsa, 1)
                look(4)
                look(5)
                act.wait_ge(s_unit, UNITS * j + 3)
                function(sg[0:FR, 2, :], ps[2][0:FR, :], ACT.Silu).then_inc(s_sil, 1)
                copy(sg[0:FR, 1, :], ps[2][FR:P, :]).then_inc(s_sil, 1)
                act_hi(EVS * j + EV_L, 0, 2, FR)

            def sweep(j, last):
                def look(m, t=0):
                    if m < UNITS:
                        split_hi(j, m, t)
                    elif not last:
                        split_hi(j + 1, m - UNITS)

                act.wait_ge(s_y1st, 16 * 2 * HQ)
                for i in range(2):
                    act.wait_ge(s_x1st[i], 16 * (C // 2) * (j + 1))
                with act.Fori(0, FT // 3 - 1) as t:
                    steps_gu(j, t, look)
                steps_gu(j, FT // 3 - 1, lambda m, t: look(m + 6 * t))
                for m in (48, 49, 50):
                    look(m)
                copy(sg[0:FR, 1, :], ps[6][FR:P, :]).then_inc(s_sil, 1)
                act.wait_ge(s_tde, 2 * (j + 1))
                copy(acts[FR:P, 0, 0, :], sg[FR:P, 0, :]).then_inc(s_hi, 1)
                for c in range(2):
                    residual_in(j, c)
                    if not last:
                        chunk_in(j + 1, c)
                for c in range(C):
                    look(DN0 + 3 * c + 3)
                    if c:
                        store(j, c - 1)
                    if not last:
                        x_hi(j + 1, c)
                    look(DN0 + 3 * c + 4)
                    if c and c + 1 < C:
                        residual_in(j, c + 1)
                    if not last and c + 2 < C:
                        chunk_free(j + 1, c)
                        chunk_in(j + 1, c + 2)
                    look(DN0 + 3 * c + 5)
                store(j, C - 1)
                if not last:
                    head(j + 1)
                for i in range(2):
                    act.wait_ge(s_out[i], 16 * (C // 2) * (j + 1))

            for m in range(NSLOT):
                split_hi(0, m, first=True)
            act.wait_ge(s_x1, HQ)
            for c in range(C):
                copy(xhi[:, c, :].rearrange("p (q n) -> p q n", q=HQ),
                     xt[:, :, c, 0:2, :].rearrange("p q g n -> p q (g n)")).then_inc(s_xhi, 1)
                act.dma_start(x1_d[:, 0, c, :].rearrange("p (q n) -> p q n", q=HQ),
                              xt[:, :, c, 0:2, :].rearrange("p q g n -> p q (g n)")).then_inc(s_x1st[c % 2], 16)
            conv_out(act, HQ - 1)
            head(0)
            with act.Fori(0, SW - 1) as j:
                sweep(j, False)
            sweep(SW - 1, True)

        @block.vector
        def _(dve):
            V = nc.vector
            count = [0]

            def step(ins):
                count[0] += 1
                ins.then_inc(s_chain, 1)
                return count[0]

            def after(n):
                dve.wait_ge(s_chain, n)

            def link(ins):
                after(step(ins))

            def together(*chains):
                last = {c: 0 for c in chains}
                while last:
                    for c in list(last):
                        if last[c]:
                            after(last[c])
                        last[c] = next(c, None)
                        if last[c] is None:
                            del last[c]
                after(count[0])

            def exp(dst, z, k, r, p, bits):
                yield step(V.tensor_scalar(p, z, 88.0, -87.0, ALU.min, ALU.max))
                yield step(V.tensor_scalar(k, p, 1.4426950408889634, MAGIC, ALU.mult, ALU.add))
                yield step(V.tensor_scalar(k, k, MAGIC, None, ALU.subtract))
                yield step(V.scalar_tensor_tensor(r, k, -LN_A, p, ALU.mult, ALU.add))
                yield step(V.scalar_tensor_tensor(r, k, -LN_B, r, ALU.mult, ALU.add))
                yield step(V.tensor_scalar(bits, k, 127.0, 8388608.0, ALU.add, ALU.mult))
                yield step(V.tensor_scalar(p, r, 1.0 / 5040, None, ALU.mult))
                for f in (720, 120, 24, 6, 2, 1):
                    yield step(V.scalar_tensor_tensor(p, p, 1.0 / f, r, ALU.add, ALU.mult))
                yield step(V.scalar_tensor_tensor(dst, p, 1.0, bits.bitcast(F32), ALU.add, ALU.mult))

            dve.wait_ge(s_in, 16 * 3)
            s = {n: sm[n][:] for n in sm}
            dt, are, aim = s["z"][:, 0:H], s["z"][:, H:2 * H], par[:, 2, :]
            together(exp(s["z"], par[:, 0:2, :].rearrange("p a h -> p (a h)"), s["ek"], s["er"], s["ep"], eki[:]))

            def angles():
                kk, v = s["kk"], s["v"]
                yield step(V.tensor_tensor(s["dim"], aim, dt, ALU.mult))
                yield step(V.tensor_scalar(kk, s["dim"], 1.0 / TWO_PI, MAGIC, ALU.mult, ALU.add))
                yield step(V.tensor_scalar(kk, kk, MAGIC, None, ALU.subtract))
                yield step(V.scalar_tensor_tensor(v, kk, -PI_A, s["dim"], ALU.mult, ALU.add))
                yield step(V.scalar_tensor_tensor(v, kk, -PI_B, v, ALU.mult, ALU.add))
                yield step(V.scalar_tensor_tensor(v, kk, -PI_C, v, ALU.mult, ALU.add))
                yield step(V.tensor_scalar(v, v, 1.0 / TWO_PI, None, ALU.mult))
                step(V.tensor_copy(s["ang"][:, 0:H], v))
                yield step(V.tensor_scalar(s["ang"][:, H:2 * H], v, 0.25, None, ALU.add))
                yield step(V.tensor_scalar(s["angk"], s["ang"], MAGIC, MAGIC, ALU.add, ALU.subtract))
                V.tensor_tensor(s["ang"], s["ang"], s["angk"], ALU.subtract).then_inc(s_small, 1)

            def decay():
                yield step(V.scalar_tensor_tensor(s["dre"], are, -1.0, dt, ALU.mult, ALU.mult))
                yield from exp(s["ed"], s["dre"], s["e2k"], s["e2r"], s["e2p"], eki[:, 0:H])

            def quotient():
                cr, ci = par[:, 3, :], par[:, 4, :]
                step(V.tensor_tensor(s["u1"], are, are, ALU.mult))
                yield step(V.tensor_tensor(s["u2"], aim, aim, ALU.mult))
                yield step(V.tensor_tensor(s["rden"], s["u1"], s["u2"], ALU.add))
                step(V.reciprocal(s["rden"], s["rden"]))
                step(V.tensor_tensor(s["u1"], cr, are, ALU.mult))
                step(V.tensor_tensor(s["u2"], ci, aim, ALU.mult))
                step(V.tensor_tensor(s["u3"], ci, are, ALU.mult))
                yield step(V.tensor_tensor(s["u4"], cr, aim, ALU.mult))
                step(V.tensor_tensor(s["qr"], s["u2"], s["u1"], ALU.subtract))
                yield step(V.scalar_tensor_tensor(s["qi"], s["u3"], -1.0, s["u4"], ALU.mult, ALU.subtract))
                step(V.tensor_tensor(s["qr"], s["qr"], s["rden"], ALU.mult))
                yield step(V.tensor_tensor(s["qi"], s["qi"], s["rden"], ALU.mult))

            together(angles(), decay(), quotient())

            def over_steps(x, g, w):
                return x[:, bass.ds(HG * g, HG)].unsqueeze(2).broadcast_to([P, HG, w])

            def over_heads(col):
                return cst[:, col:col + 2 * NA].unsqueeze(1).broadcast_to([P, HG, 2 * NA])

            STEPS = 9
            t = {n: tb[n][:] for n in tb} | {n: th[n][:] for n in th}

            class Group:
                def __init__(self, g, base):
                    self.g, self.base, self.n = g, base, 0

                def link(self, ins):
                    ins.then_inc(s_chain, 1)
                    self.n += 1
                    dve.wait_ge(s_chain, self.base + STEPS * self.g + self.n)

            def arguments(grp):
                g = grp.g
                V.tensor_tensor(t["q"], over_steps(s["dre"], g, 2 * NA), over_heads(CAB), ALU.mult).then_inc(s_arg, 1)
                grp.link(V.tensor_tensor(t["p"], over_steps(s["v"], g, 2 * NA), over_heads(CAB), ALU.mult))
                grp.link(V.tensor_scalar(t["k"], t["p"], MAGIC, MAGIC, ALU.add, ALU.subtract))
                grp.link(V.tensor_tensor(t["f"], t["p"], t["k"], ALU.subtract))
                grp.link(V.tensor_tensor(t["g"], t["f"], over_heads(CPH), ALU.add))
                grp.link(V.tensor_scalar(t["k"], t["g"], MAGIC, MAGIC, ALU.add, ALU.subtract))
                V.tensor_tensor(t["f3"], t["g"], t["k"], ALU.subtract).then_inc(s_arg, 1)

            def products(grp, wait_prev):
                g = grp.g
                dve.wait_ge(s_trig, 3 * g + 3)
                V.tensor_tensor(t["t1"], t["tr"][:, :, 0:NA], over_steps(s["c1"], g, NA), ALU.mult).then_inc(s_chain, 1)
                grp.n += 1
                grp.link(V.tensor_tensor(t["t2"], t["s1"], over_steps(s["c2"], g, NA), ALU.mult))
                grp.link(V.tensor_tensor(t["t1"], t["t1"], t["t2"], ALU.add))
                if wait_prev:
                    dve.wait_ge(s_kmm, g)
                V.tensor_tensor(t["gg"], t["t1"], t["m"][:, :, 0:NA], ALU.mult)
                V.tensor_tensor(t["e2"], t["tr"][:, :, NA:2 * NA], t["m"][:, :, NA:2 * NA], ALU.mult).then_inc(s_tab, 1)

            def k_out(grp, wait_store):
                g = grp.g
                dve.wait_ge(s_kmm, g + 1)
                if wait_store:
                    dve.wait_ge(s_kst, 16 * g)
                grp.link(V.tensor_copy(ksb[0:NA, :, :].rearrange("p h b -> p (h b)"), ps[7][0:NA, 0:HG * NA]))
                assert grp.n == STEPS
                dst = ksb[0:1, :, 0:1].rearrange("p h b -> p (h b)")
                V.tensor_tensor(dst, dst, par[0:1, 5, bass.ds(HG * g, HG)], ALU.add).then_inc(s_ksb, 1)

            COEF = 13
            first = Group(0, count[0])
            arguments(first)
            count[0] += first.n
            c0 = count[0]
            dve.wait_ge(s_smallA, 1)
            sn, cs = s["trig"][:, 0:H], s["trig"][:, H:2 * H]
            step(V.tensor_tensor(s["ei"], s["ed"], sn, ALU.mult))
            link(V.tensor_tensor(s["er1"], s["ed"], cs, ALU.mult))
            link(V.tensor_scalar(s["er1"], s["er1"], 1.0, None, ALU.subtract))
            step(V.tensor_tensor(s["u1"], s["qr"], s["er1"], ALU.mult))
            step(V.tensor_tensor(s["u2"], s["qi"], s["ei"], ALU.mult))
            step(V.tensor_tensor(s["u3"], s["qr"], s["ei"], ALU.mult))
            link(V.tensor_tensor(s["u4"], s["qi"], s["er1"], ALU.mult))
            step(V.tensor_tensor(s["cr"], s["u1"], s["u2"], ALU.subtract))
            link(V.tensor_tensor(s["ci"], s["u3"], s["u4"], ALU.add))
            al, be, nal = (cst[:, x:x + 1] for x in (CAL, CBE, CNAL))
            step(V.tensor_scalar(s["u1"], s["ci"], be, None, ALU.mult))
            link(V.tensor_scalar(s["u2"], s["cr"], be, None, ALU.mult))
            step(V.scalar_tensor_tensor(s["c1"], s["cr"], al, s["u1"], ALU.mult, ALU.add))
            link(V.scalar_tensor_tensor(s["c2"], s["ci"], nal, s["u2"], ALU.mult, ALU.add))
            assert count[0] - c0 == COEF
            first.base += COEF
            products(first, False)
            V.tensor_copy(lenf[:, :], leni[:, :]).then_inc(s_len, 1)
            dve.wait_ge(s_len, 1)
            for c in range(C):
                V.tensor_scalar(mask[:, c, :], lenf[:, :], cst[:, CPOS + c:CPOS + c + 1], None,
                                ALU.is_gt).then_inc(s_len, 1)
            dve.wait_ge(s_len, 1 + C)
            k_out(first, False)
            base = first.base

            def group(g):
                return Group(g, base)

            grp = group(1)
            arguments(grp)
            products(grp, True)
            k_out(grp, True)

            def evacuate(hq, i):
                dve.wait_ge(s_conv, HH * hq + i + 1)
                out = xt[:, bass.ds(hq, 1), :, :, i * BG:(i + 1) * BG].rearrange("p q c g b -> p (q c) g b")
                V.tensor_tensor(out, ps[i % NCV][:, 0:C * B].rearrange("p (c g b) -> p c g b", c=C, g=G),
                                mask[:].rearrange("p c (g b) -> p c g b", g=G), ALU.mult).then_inc(s_cev, 1)

            def split_lo(j, m, t=0):
                slot, w = m % NSLOT, tiles_of(m)
                dve.wait_ge(s_whi, UNITS * j + m + 6 * t + 1)
                if TD0 <= m < DN0:
                    dve.wait_ge(s_tdh, 3 * j + m - TD0 + 1)
                    for g, (out, sm_) in enumerate(((whi, s_tdl), (wlo, s_wlo))):
                        V.tensor_tensor(down_rows(out, slot, w, FR), down_raw(slot, w, g),
                                        down_rows(out, slot, w, 0).bitcast(F32), ALU.subtract).then_inc(sm_, 1)
                elif m < 2:
                    V.tensor_tensor(gate_up_tiles(wlo, slot), gate_up_raw(slot),
                                    gate_up_tiles(whi, slot).bitcast(F32), ALU.subtract).then_inc(s_wlo, 1)
                else:
                    V.tensor_tensor(wlo[:, slot, 0:w * P], raw[:, slot, 0:w * P],
                                    whi[:, slot, 0:w * P].bitcast(F32), ALU.subtract).then_inc(s_wlo, 1)

            def x1_rows(hq):
                dve.wait_ge(s_cev, HH * (hq + 1))
                dve.wait_ge(s_x0, 16 * HQ)
                rows = xt[:, bass.ds(hq, 1), :, 0:2, :].rearrange("p q c g n -> p (q c) (g n)")
                V.tensor_tensor(rows, rows, xn0[:, bass.ds(hq, 1)].rearrange("p q c n -> p (q c) n"),
                                ALU.add).then_inc(s_x1, 1)

            with dve.Fori(0, HQ - 1) as hq:
                for half in range(2):
                    grp = group(2 * hq + half + 2)
                    for i in range(half * HG, half * HG + HG // 2):
                        evacuate(hq, i)
                    arguments(grp)
                    for i in range(half * HG + HG // 2, half * HG + 6):
                        evacuate(hq, i)
                    products(grp, True)
                    for i in range(half * HG + 6, (half + 1) * HG):
                        evacuate(hq, i)
                    k_out(grp, True)
            for i in range(HH):
                evacuate(HQ - 1, i)
                if i in (5, 7, 9):
                    x1_rows((i - 5) // 2)
                if i == HH - 4:
                    dve.wait_ge(s_x1, HQ - 1)
                    split_lo(0, 0)
            x1_rows(HQ - 1)

            def x_lo(j, c):
                dve.wait_ge(s_xn[c % 2], 16 * (C // 2) * (j - 1) + 16 * (c // 2 + 1))
                dve.wait_ge(s_y1[c % 2], 16 * (C // 2) * (j - 1) + 16 * (c // 2 + 1))
                V.tensor_tensor(y1s[:, c % 2, :], y1s[:, c % 2, :], xns[:, c % 2, :], ALU.add).then_inc(s_xsum, 1)
                dve.wait_ge(s_xhi, C * j + c + 1)
                V.tensor_tensor(xlo[:, c, :], y1s[:, c % 2, :], xhi[:, c, :].bitcast(F32),
                                ALU.subtract).then_inc(s_xlo, 1)

            def by_batch(x):
                return x.rearrange("p (n b) -> p n b", b=BG)

            def lora_mask(rows):
                return cst[rows, CMASK:CMASK + BG].unsqueeze(1).broadcast_to([rows.stop - rows.start, T // BG, BG])

            def act_lo(hi_count, slot, i3, rows=P):
                dve.wait_ge(s_hi, hi_count)
                tile = acts[0:rows, bass.ds(slot, 1), :, :].rearrange("p a h n -> p (a h) n")
                V.tensor_tensor(tile[:, 1, :], sg[0:rows, i3, :], tile[:, 0, :].bitcast(F32),
                                ALU.subtract).then_inc(s_act, 1)

            def steps_gu(j, t_, look):
                for q in range(6):
                    m = GU0 + 1 + q
                    look(m + 2, t_)
                    if q % 2:
                        i3, bank = q // 2, (GU0 + q) % 6
                        dve.wait_ge(s_unit, UNITS * j + m + 6 * t_)
                        dve.wait_ge(s_sil, SIL * j + 2 + 3 * t_ + i3 + 1)
                        V.tensor_tensor(sg[:, i3, :], sg[:, i3, :], ps[bank][:, :], ALU.mult).then_inc(s_ev, 1)
                        act_lo(HIS * j + 2 + 3 * t_ + i3 + 1, 3 * t_ + i3 + 1, i3)

            def sweep(j, last):
                def look(m, t_=0):
                    if m < UNITS:
                        split_lo(j, m, t_)
                    elif not last:
                        split_lo(j + 1, m - UNITS)

                look(3)
                dve.wait_ge(s_unit, UNITS * j + 2)
                V.tensor_tensor(by_batch(sg[:, 0, :]), by_batch(ps[0][:, :]), lora_mask(slice(0, P)),
                                ALU.mult).then_inc(s_ev, 1)
                dve.wait_ge(s_hi, HIS * j + 1)
                V.tensor_tensor(tlo[:, :], sg[:, 0, :], thi[:, :].bitcast(F32), ALU.subtract).then_inc(s_t, 1)
                for half in range(2):
                    rows = slice(half * FR, (half + 1) * FR)
                    V.tensor_tensor(ts[FR:P, half, :], sg[rows, 0, :], thi[rows, :].bitcast(F32),
                                    ALU.subtract).then_inc(s_tsd, 1)
                    V.tensor_copy(tz[0:FR, half, :], thi[rows, :].bitcast(F32)).then_inc(s_tsd, 1)
                look(4)
                look(5)
                dve.wait_ge(s_sil, SIL * j + 2)
                V.tensor_tensor(sg[0:FR, 2, :], sg[0:FR, 2, :], sg[0:FR, 1, :], ALU.mult).then_inc(s_ev, 1)
                act_lo(HIS * j + 2, 0, 2, FR)
                with dve.Fori(0, FT // 3 - 1) as t_:
                    steps_gu(j, t_, look)
                steps_gu(j, FT // 3 - 1, lambda m, t_: look(m + 6 * t_))
                for m in (48, 49, 50):
                    look(m)
                dve.wait_ge(s_unit, UNITS * j + DN0)
                dve.wait_ge(s_sil, SIL * (j + 1))
                V.tensor_tensor(sg[0:FR, 1, :], ps[6][0:FR, :], sg[0:FR, 1, :], ALU.add).then_inc(s_tde, 1)
                dve.wait_ge(s_tde, 2 * j + 1)
                V.tensor_tensor(by_batch(sg[FR:P, 0, :]), by_batch(sg[0:FR, 1, :]), lora_mask(slice(0, FR)),
                                ALU.mult).then_inc(s_tde, 1)
                dve.wait_ge(s_hi, HIS * (j + 1))
                V.tensor_tensor(acts[FR:P, 0, 1, :], sg[FR:P, 0, :], acts[FR:P, 0, 0, :].bitcast(F32),
                                ALU.subtract).then_inc(s_td, 1)
                for c in range(C):
                    if not last:
                        x_lo(j + 1, c)
                    for m in range(DN0 + 3 * c + 3, DN0 + 3 * c + 6):
                        look(m)
                    dve.wait_ge(s_unit, UNITS * j + DN0 + 3 * c + 3)
                    dve.wait_ge(s_xres[c % 2], 16 * (C // 2) * j + 16 * (c // 2 + 1))
                    V.tensor_tensor(xres[:, c % 2, :], ps[7 - c % 2][:, :], xres[:, c % 2, :],
                                    ALU.add).then_inc(s_ev, 1)

            dve.wait_ge(s_x1, HQ)
            for c in range(C):
                if c in (3, 6):
                    split_lo(0, c // 3)
                dve.wait_ge(s_xhi, c + 1)
                V.tensor_tensor(xlo[:, c, :].rearrange("p (q n) -> p q n", q=HQ),
                                xt[:, :, c, 0:2, :].rearrange("p q g n -> p q (g n)"),
                                xhi[:, c, :].rearrange("p (q n) -> p q n", q=HQ).bitcast(F32),
                                ALU.subtract).then_inc(s_xlo, 1)
            V.memset(tz[FR:P, :, :].bitcast(F32), 0.0).then_inc(s_tz, 1)
            with dve.Fori(0, SW - 1) as j:
                sweep(j, False)
            sweep(SW - 1, True)


def constants():
    p = np.arange(P)
    cst = np.zeros((P, NC_), np.float32)
    cst[:, CAB:CAB + NA] = NA * np.arange(NA)
    cst[:, CAB + NA:CAB + 2 * NA] = np.arange(NA)
    cst[:, CPH:CPH + NA] = 0.25
    cst[:, CPH + NA:CPH + 2 * NA] = np.where(p < NS, 0.25, 0.0)[:, None]
    cst[:, CPOS:CPOS + C] = P * np.arange(C)[None, :] + p[:, None]
    cst[:, CMASK:CMASK + BG] = 0.5 * (p[:, None] // RANK % BG == np.arange(BG)[None, :])
    cst[:, CAL] = np.where(p < NS, 2.0, 0.0)
    cst[:, CBE] = np.where(p < NS, 0.0, -2.0)
    cst[:, CNAL] = -cst[:, CAL]
    return cst


def layouts(x, itok_B_8_3872, itok_B_2_6, L0_cond_log_dt, L0_cond_C, L0_cond_log_A_real, L0_cond_A_imag,
            L0_cond_D, L1_cond_W_gate, L1_cond_W_up, L1_cond_W_down, L1_cond_A_gate, L1_cond_B_gate,
            L1_cond_A_up, L1_cond_B_up, L1_cond_A_down, L1_cond_B_down):
    c = np.ascontiguousarray
    a = {}
    xs = np.asarray(x).reshape(SW, 2, BG, HQ, HH, C, P)
    a["xt"] = c(xs.transpose(6, 3, 5, 0, 1, 4, 2)[::-1].reshape(P, HQ, C, G, HT))
    a["xn"] = c(xs.transpose(6, 0, 5, 3, 1, 4, 2).reshape(P, SW, C, T))
    a["idx"] = c(np.asarray(itok_B_2_6).reshape(1, B))
    a["len"] = c(np.asarray(itok_B_8_3872).reshape(1, B))
    rows = lambda v: np.broadcast_to(np.asarray(v)[None, :], (P, H))
    twice = lambda m: np.concatenate([np.asarray(m).T, np.asarray(m).T], 0)
    Cc = np.asarray(L0_cond_C)
    a["par"] = c(np.stack([rows(L0_cond_log_dt), twice(L0_cond_log_A_real), twice(L0_cond_A_imag),
                           twice(Cc[..., 0]), twice(Cc[..., 1]), rows(L0_cond_D)], 1))
    a["cst"] = constants()
    FW = FT * P
    tiles = lambda w: np.asarray(w)[:FW].reshape(FT, P, C, P).transpose(0, 3, 2, 1).reshape(FT, P, C * P)
    wg, wu = np.asarray(L1_cond_W_gate), np.asarray(L1_cond_W_up)
    a["wgu"] = c(np.concatenate([tiles(wg), tiles(wu)], 2))
    rest = lambda w: w[FW:].reshape(FR, C, P).transpose(2, 1, 0)
    a["wl"] = c(np.concatenate([rest(wg), rest(wu)], 2).reshape(P, C * P))
    bg, bu = (np.asarray(v)[0].transpose(0, 2, 1) for v in (L1_cond_B_gate, L1_cond_B_up))
    a["bgu"] = c(np.stack([v[:, :, :FW].reshape(R, RANK, FT, P).transpose(0, 2, 1, 3) for v in (bg, bu)], 3))
    bl = np.zeros((R, 2, RANK, P), np.float32)
    bl[:, 0, :, 0:FR] = bg[:, :, FW:]
    bl[:, 1, :, FR:P] = bu[:, :, FW:]
    a["bl"] = bl
    wd = np.asarray(L1_cond_W_down)
    a["wd"] = c(wd[:, :FW].reshape(C, P, FT, P).transpose(0, 3, 2, 1).reshape(C, P, FT * P))
    wdl = wd[:, FW:].reshape(C, P, FR).transpose(0, 2, 1)
    a["wdl"] = c(np.stack([wdl, wdl], 2))
    bd = np.asarray(L1_cond_B_down)[0]
    a["bd"] = c(bd.reshape(R, C, P, RANK).transpose(0, 1, 3, 2))
    amat = lambda v: np.asarray(v)[0].reshape(R, RANK, C, P).transpose(0, 3, 2, 1)
    a["agu"] = c(np.stack([amat(L1_cond_A_gate), amat(L1_cond_A_up)], 3).reshape(R, P, C * 2 * RANK))
    ad = np.zeros((R, P, KT, RANK), np.float32)
    v = np.asarray(L1_cond_A_down)[0]
    ad[:, :, :FT] = v[:, :, :FW].reshape(R, RANK, FT, P).transpose(0, 3, 2, 1)
    ad[:, :FR, FT] = v[:, :, FW:].transpose(0, 2, 1)
    a["ad"] = ad.reshape(R, P, KT * RANK)
    return a


ORDER = ("xt", "xn", "idx", "len", "par", "cst", "wgu", "wl", "bgu", "bl", "wd", "wdl", "bd", "agu", "ad")


def kernel(**inputs):
    import concourse.bacc as bacc
    from concourse.bass_utils import run_bass_kernel_spmd
    arrays = layouts(**inputs)
    nc = bacc.Bacc("TRN2", target_bir_lowering=False, num_devices=1)
    args = [nc.dram_tensor(n, arrays[n].shape, mybir.dt.from_np(arrays[n].dtype), kind="ExternalInput").ap()
            for n in ORDER]
    out = nc.dram_tensor("out", (P, SW, C, T), F32, kind="ExternalOutput").ap()
    build(nc, *args, out)
    r = run_bass_kernel_spmd(nc, [arrays], core_ids=[0])
    y = r.results[0]["out"].reshape(P, SW, C, HQ, 2, HH, BG)
    return np.ascontiguousarray(y.transpose(1, 4, 6, 3, 5, 2, 0)).reshape(B, H, L)
```
